# Optimizing a Trainium2 kernel written in Bass

```python
import numpy as np
import jax
import jax.numpy as jnp

def _softmax(x, axis=-1):
    return jax.nn.softmax(x, axis=axis)

def _gelu(x):
    return jax.nn.gelu(x, approximate=True)

def _silu(x):
    return jax.nn.silu(x)

def _sigmoid(x):
    return jax.nn.sigmoid(x)

def _layernorm(x, axis=-1, eps=1e-05):
    m = jnp.mean(x, axis=axis, keepdims=True)
    v = jnp.var(x, axis=axis, keepdims=True)
    return (x - m) / jnp.sqrt(v + eps)

def _scatter_add(tgt, idx, src, axis=0):
    return tgt.at[idx].add(src)

def _segment_sum(src, seg, n):
    return jax.ops.segment_sum(src, seg, n)
kernel_name = 'mk_gnn_preln_d1_gnn_r8_2f9736'

def setup_inputs(seed: int=0):
    np.random.seed(seed)
    _w = jnp.asarray

    def _rec_inputs():
        import jax
        import jax.numpy as jnp
        _gk = jax.random.key(seed)
        x = -1.686e-05 + 1 * jax.random.normal(jax.random.fold_in(_gk, 1), (6250, 160), jnp.float32)
        _s = jax.random.randint(jax.random.fold_in(_gk, 2), (100000,), 0, 6250, jnp.int32)
        _d = jax.random.randint(jax.random.fold_in(_gk, 3), (100000,), 0, 6250, jnp.int32)
        _loop = jnp.arange(6250, dtype=jnp.int32)
        src = jnp.concatenate([_s, _d, _loop])
        dst = jnp.concatenate([_d, _s, _loop])
        _o = jnp.argsort(dst, stable=True)
        src = src[_o]
        dst = dst[_o]
        edge_attr_10 = jax.random.uniform(jax.random.fold_in(_gk, 12), (206250, 10), jnp.float32, 0.0, 1)
        edge_attr_4 = -0.000107899 + 1.00008 * jax.random.normal(jax.random.fold_in(_gk, 13), (206250, 4), jnp.float32)
        node_vec1 = jax.random.uniform(jax.random.fold_in(_gk, 14), (6250, 1), jnp.float32, 0.0, 1)
        return (x, src, dst, edge_attr_10, edge_attr_4, node_vec1)
    x, src, dst, edge_attr_10, edge_attr_4, node_vec1 = _rec_inputs()

    def _L0_gnn_setup():
        import jax, jax.numpy as jnp
        import numpy as np
        N_NODES = 6250
        N_EDGES = 100000
        MUL0, MUL1 = (64, 32)
        N_BASIS, N_RADIAL = (10, 100)
        W_NUMEL = 192
        NUM_NEIGHBORS = 16.0
        INV_SQRT3 = np.float32(1.0 / np.sqrt(3.0))
        RELU_GAIN = np.float32(np.sqrt(2.0))
        FAN_L2 = np.float32(np.sqrt(MUL0 + MUL1))

        def _fctp_scalar_attr(x0, x1, a, W0, W1):
            o0 = x0 @ W0 * a * (1.0 / np.sqrt(W0.shape[0]))
            o1 = jnp.einsum('nud,uw->nwd', x1, W1) * a[..., None] * (1.0 / np.sqrt(W1.shape[0]))
            return (o0, o1)
        key = jax.random.key(seed)
        ks = jax.random.split(key, 16)
        return {'node_input': jax.random.normal(ks[0], (N_NODES, MUL0 + 3 * MUL1), jnp.float32), 'node_attr': jnp.ones((N_NODES, 1), jnp.float32), 'edge_attr': jax.random.normal(ks[1], (N_EDGES, 4), jnp.float32), 'edge_length_embedded': jax.random.uniform(ks[2], (N_EDGES, N_BASIS), dtype=jnp.float32), 'W_si0': jax.random.normal(ks[3], (MUL0, MUL0), jnp.float32), 'W_si1': jax.random.normal(ks[4], (MUL1, MUL1), jnp.float32), 'W_l1_0': jax.random.normal(ks[5], (MUL0, MUL0), jnp.float32), 'W_l1_1': jax.random.normal(ks[6], (MUL1, MUL1), jnp.float32), 'W_l2_00': jax.random.normal(ks[7], (MUL0, MUL0), jnp.float32), 'W_l2_10': jax.random.normal(ks[8], (MUL1, MUL0), jnp.float32), 'W_l2_01': jax.random.normal(ks[9], (MUL0, MUL1), jnp.float32), 'W_l2_11': jax.random.normal(ks[10], (MUL1, MUL1), jnp.float32), 'W_fc1': jax.random.normal(ks[11], (N_BASIS, N_RADIAL), jnp.float32), 'W_fc2': jax.random.normal(ks[12], (N_RADIAL, W_NUMEL), jnp.float32), 'edge_src': jax.random.randint(ks[13], (N_EDGES,), 0, N_NODES), 'edge_dst': jax.random.randint(ks[14], (N_EDGES,), 0, N_NODES)}
    _L0_gnn_all = _L0_gnn_setup()
    _L0_gnn_in = {k: v for k, v in _L0_gnn_all.items() if k in ('W_si0', 'W_si1', 'W_l1_0', 'W_l1_1', 'W_l2_00', 'W_l2_10', 'W_l2_01', 'W_l2_11', 'W_fc1', 'W_fc2')}
    del _L0_gnn_all
    return {'x': x, 'src': src, 'dst': dst, 'edge_attr_10': edge_attr_10, 'edge_attr_4': edge_attr_4, 'node_vec1': node_vec1, 'L0_gnn_W_si0': _L0_gnn_in['W_si0'], 'L0_gnn_W_si1': _L0_gnn_in['W_si1'], 'L0_gnn_W_l1_0': _L0_gnn_in['W_l1_0'], 'L0_gnn_W_l1_1': _L0_gnn_in['W_l1_1'], 'L0_gnn_W_l2_00': _L0_gnn_in['W_l2_00'], 'L0_gnn_W_l2_10': _L0_gnn_in['W_l2_10'], 'L0_gnn_W_l2_01': _L0_gnn_in['W_l2_01'], 'L0_gnn_W_l2_11': _L0_gnn_in['W_l2_11'], 'L0_gnn_W_fc1': _L0_gnn_in['W_fc1'], 'L0_gnn_W_fc2': _L0_gnn_in['W_fc2']}

def reference(x, src, dst, edge_attr_10, edge_attr_4, node_vec1, L0_gnn_W_si0, L0_gnn_W_si1, L0_gnn_W_l1_0, L0_gnn_W_l1_1, L0_gnn_W_l2_00, L0_gnn_W_l2_10, L0_gnn_W_l2_01, L0_gnn_W_l2_11, L0_gnn_W_fc1, L0_gnn_W_fc2):
    import jax
    import jax.numpy as jnp

    def _L0_gnn_ref(node_input, node_attr, edge_src, edge_dst, edge_attr, edge_length_embedded, W_si0, W_si1, W_l1_0, W_l1_1, W_l2_00, W_l2_10, W_l2_01, W_l2_11, W_fc1, W_fc2):
        import jax, jax.numpy as jnp
        import numpy as np
        N_NODES = 6250
        N_EDGES = 100000
        MUL0, MUL1 = (64, 32)
        N_BASIS, N_RADIAL = (10, 100)
        W_NUMEL = 192
        NUM_NEIGHBORS = 16.0
        INV_SQRT3 = np.float32(1.0 / np.sqrt(3.0))
        RELU_GAIN = np.float32(np.sqrt(2.0))
        FAN_L2 = np.float32(np.sqrt(MUL0 + MUL1))

        def _fctp_scalar_attr(x0, x1, a, W0, W1):
            o0 = x0 @ W0 * a * (1.0 / np.sqrt(W0.shape[0]))
            o1 = jnp.einsum('nud,uw->nwd', x1, W1) * a[..., None] * (1.0 / np.sqrt(W1.shape[0]))
            return (o0, o1)
        N = node_input.shape[0]
        x0 = node_input[:, :MUL0]
        x1 = node_input[:, MUL0:].reshape(N, MUL1, 3)
        a = node_attr
        h = jax.nn.relu(edge_length_embedded @ W_fc1 * (1.0 / np.sqrt(N_BASIS))) * RELU_GAIN
        w = h @ W_fc2 * (1.0 / np.sqrt(N_RADIAL))
        w0, w1, w2, w3 = (w[:, :64], w[:, 64:128], w[:, 128:160], w[:, 160:192])
        si0, si1 = _fctp_scalar_attr(x0, x1, a, W_si0, W_si1)
        l0, l1 = _fctp_scalar_attr(x0, x1, a, W_l1_0, W_l1_1)
        y0 = l0[edge_src]
        y1 = l1[edge_src]
        e0 = edge_attr[:, :1]
        e1 = edge_attr[:, 1:4]
        m0 = w0 * y0 * e0
        m1 = (w1 * y0)[:, :, None] * e1[:, None, :]
        m2 = (w2 * e0)[:, :, None] * y1
        m3 = w3 * jnp.einsum('eud,ed->eu', y1, e1) * INV_SQRT3
        inv = np.float32(1.0 / np.sqrt(NUM_NEIGHBORS))
        s0 = jax.ops.segment_sum(m0, edge_dst, num_segments=N) * inv
        s1 = jax.ops.segment_sum(m1, edge_dst, num_segments=N) * inv
        s2 = jax.ops.segment_sum(m2, edge_dst, num_segments=N) * inv
        s3 = jax.ops.segment_sum(m3, edge_dst, num_segments=N) * inv
        o0 = (s0 @ W_l2_00 + s3 @ W_l2_10) * a / FAN_L2
        o1 = (jnp.einsum('nud,uw->nwd', s1, W_l2_01) + jnp.einsum('nud,uw->nwd', s2, W_l2_11)) * a[..., None] / FAN_L2
        out0 = si0 + 0.5 * o0
        out1 = si1 + 0.5 * o1
        return jnp.concatenate([out0, out1.reshape(N, 3 * MUL1)], axis=1)
    h = jnp.maximum(_layernorm(x, axis=-1), 0.0)
    x = x + _L0_gnn_ref(h, node_vec1, src, dst, edge_attr_4, edge_attr_10, L0_gnn_W_si0, L0_gnn_W_si1, L0_gnn_W_l1_0, L0_gnn_W_l1_1, L0_gnn_W_l2_00, L0_gnn_W_l2_10, L0_gnn_W_l2_01, L0_gnn_W_l2_11, L0_gnn_W_fc1, L0_gnn_W_fc2)
    return x

_drawn_inputs = setup_inputs


def setup_inputs(seed=0):
    import zlib

    import numpy as np

    out = dict(_drawn_inputs(seed))
    spreads = {}
    factors = {}
    for name, (base, spread) in spreads.items():
        noise = np.random.default_rng([zlib.crc32(name.encode()), seed]).standard_normal(out[name].shape)
        drawn = base * np.exp(spread * noise) if base else spread * noise
        out[name] = jnp.asarray(drawn.astype(out[name].dtype))
    for name, factor in factors.items():
        out[name] = (out[name] * factor).astype(out[name].dtype)
    return out
```

```python
import numpy as np
import concourse.bass as bass
from concourse import mybir
from contextlib import ExitStack

P = 128
N = 6250
E = 206250
MUL0, MUL1 = 64, 32
C = MUL0 + 3 * MUL1
N_BASIS, N_RADIAL = 10, 100
NW = 2 * MUL0 + 2 * MUL1
BLOCKS = -(-N // P)
CHUNK = 7
CHUNKS = BLOCKS // CHUNK
assert CHUNKS * CHUNK == BLOCKS
NP = BLOCKS * P

T = 4
W = 32
V = 5
G = 4
HALF = 2
TURNS = -(-E // (P * T * G))
GROUPS = TURNS * G
TILES = GROUPS * T
EP = TILES * P
GE = T * P
NA = N + W
M = 2 * P
TRASH = NP
ND = NP + P

EPS = 1e-5
K_RADIAL = float(np.sqrt(2.0) / np.sqrt(N_BASIS))
K_SUM = float(0.5 / np.sqrt(16.0) / np.sqrt(MUL0 + MUL1) / np.sqrt(N_RADIAL))
K_DOT = float(1.0 / np.sqrt(3.0))

F32 = mybir.dt.float32
I32 = mybir.dt.int32
ALU = mybir.AluOpType
ACT = mybir.ActivationFunctionType
AX = mybir.AxisListType


def gnn_layer(nc, x, src, dst, radial, attr, avec, wsi0, wsi1, wl0, wl1, w00, w10, w01, w11, wf1, wf2, out):
    ctx = ExitStack()
    with ctx:
        def sb(name, shape, dt=F32):
            return ctx.enter_context(nc.sbuf_tensor(name, shape, dt))

        def sem(name):
            return ctx.enter_context(nc.semaphore(name))

        table = nc.dram_tensor("table", (NP, C), F32).ap()
        sums_d = nc.dram_tensor("sums_d", (ND, 4 * P), F32).ap()

        acc = sb("acc", [P, 4, NA])
        xres = sb("xres", [P, BLOCKS, C])
        a_sb = sb("a_sb", [P, BLOCKS])
        dst_i = sb("dst_i", [P, TILES], I32)
        dst_rel = sb("dst_rel", [P, TILES])
        base_f = sb("base_f", [1, GROUPS])
        base_i = sb("base_i", [1, GROUPS], I32)
        iota_i = sb("iota_i", [P, W], I32)
        iota_w = sb("iota_w", [P, W])
        ident = sb("ident", [P, P])
        ones = sb("ones", [P, P])
        span = sb("span", [P, 4])
        flag_i = sb("flag_i", [1, 1], I32)
        wnode = sb("wnode", [P, 2, P])
        wnode_z = sb("wnode_z", [MUL1, 2, MUL1])
        w_fc1 = sb("w_fc1", [N_BASIS, N_RADIAL])
        w_fc2 = sb("w_fc2", [N_RADIAL, NW])
        w_out = sb("w_out", [P, 4, C])
        stats = sb("stats", [P, CHUNK, 6])
        mean_var = sb("mean_var", [P, CHUNK, 2])
        eps = sb("eps", [P, 1])
        std = sb("std", [P, CHUNK])
        rstd = sb("rstd", [P, CHUNK])
        shift = sb("shift", [P, CHUNK])
        hid = sb("hid", [P, CHUNK, C])
        hid_t = sb("hid_t", [P, CHUNK, 2, P])
        l_st = sb("l_st", [P, CHUNK, C])
        idx = sb("idx", [P, 2, HALF * T], I32)
        attr_sb = sb("attr_sb", [P, 2, HALF * T, 4])
        rad = sb("rad", [N_BASIS, 2, HALF * GE])
        y = sb("y", [P, G, T, C])
        hr = sb("hr", [N_RADIAL, 2, GE])
        msg = sb("msg", [P, 2, T, M])
        hot = sb("hot", [P, 2, T, V, W])
        dots = sb("dots", [P, T, 3, MUL1])
        dot = sb("dot", [P, T, MUL1])
        fin_in = msg[:, :, :, :].rearrange("p s t m -> p s (t m)")[:, :, 0:4 * P]
        spare = msg[:, 1, :, :].rearrange("p t m -> p (t m)")
        full, sums = spare[:, 0:4 * P], spare[:, 4 * P:8 * P]
        spare = hot[:, 1, :, :, :].rearrange("p t v w -> p (t v w)")
        same, same_before, dst_bc = (spare[:, n * P:(n + 1) * P] for n in range(3))
        lower = sb("lower", [P, P])
        dst_col = sb("dst_col", [P, 1])
        repeats = sb("repeats", [P, 1])
        trash_i = sb("trash_i", [P, 1], I32)
        trash = sb("trash", [P, 1])
        away = sb("away", [P, 1])
        idx_sum = sb("idx_sum", [P, 1], I32)
        rows_in = y[:, 0, :, :].rearrange("p t c -> p (t c)")[:, 0:4 * P]

        def ps(name, shape):
            return ctx.enter_context(nc.psum_tensor(name, shape, F32))

        ps_h = ps("ps_h", [P, 2, 512])
        ps_w = ps("ps_w", [P, 2, T, 256])
        ps_s = ps("ps_s", [P, 2, 512])

        sp_passed, dve_passed, pool_passed = sem("sp_passed"), sem("dve_passed"), sem("pool_passed")
        ld_x = sem("ld_x")
        ld_dst = sem("ld_dst")
        ld_a = sem("ld_a")
        ld_w = sem("ld_w")
        zeroed = sem("zeroed")
        consts = sem("consts")
        dst_step = sem("dst_step")
        base_bc = sem("base_bc")
        flag_sum = sem("flag_sum")
        flag_set = sem("flag_set")
        w_scaled = sem("w_scaled")
        bn_done = sem("bn_done")
        aggr_done = sem("aggr_done")
        std_done = sem("std_done")
        rstd_done = sem("rstd_done")
        norm_done = sem("norm_done")
        hid_done = sem("hid_done")
        tr_done = sem("tr_done")
        hidt_a = sem("hidt_a")
        hidt_b = sem("hidt_b")
        node_mm = sem("node_mm")
        l_done = sem("l_done")
        res_done = sem("res_done")
        table_out = sem("table_out")
        ld_idx = [sem(f"ld_idx{c}") for c in range(2)]
        ld_attr = [sem(f"ld_attr{c}") for c in range(2)]
        ld_rad = [sem(f"ld_rad{c}") for c in range(2)]
        gathered = [sem(f"gathered{j}") for j in range(G)]
        fc1_done = sem("fc1_done")
        relu_done = sem("relu_done")
        fc2_done = sem("fc2_done")
        hot_done = sem("hot_done")
        dots_done = sem("dots_done")
        dot_done = sem("dot_done")
        msg_done = sem("msg_done")
        win_done = sem("win_done")
        acc_done = sem("acc_done")
        path_done = sem("path_done")
        g_zeroed, g_free, g_loaded, g_rows, g_fc1, g_relu, g_fc2 = (
            sem("g_" + n) for n in ("zeroed", "free", "loaded", "rows", "fc1", "relu", "fc2"))
        g_col, g_turned, g_full, g_summed, g_taken, g_added, g_turn = (
            sem("g_" + n) for n in ("col", "turned", "full", "summed", "taken", "added", "turn"))
        g_block_free, g_block_in, g_block_turned = (sem("g_block_" + n) for n in ("free", "in", "turned"))
        fin_copied = sem("fin_copied")
        fin_mm = sem("fin_mm")
        fin_done = sem("fin_done")
        stored = sem("stored")

        table_v = table.rearrange("(b p) c -> p b c", p=P)
        x_v = x.rearrange("(b p) c -> p b c", p=P)
        out_v = out.rearrange("(b p) c -> p b c", p=P)

        weight_loads = [(w_fc1[:, :], wf1), (w_fc2[:, :], wf2),
                        (wnode[0:MUL0, 0, 0:MUL0], wl0), (wnode[0:MUL0, 1, 0:MUL0], wsi0),
                        (wnode_z[:, 0, :], wl1), (wnode_z[:, 1, :], wsi1),
                        (w_out[0:MUL0, 0, 0:MUL0], w00), (w_out[3 * MUL1:P, 3, 0:MUL0], w10)]
        for d in range(2):
            at = slice(MUL0 + MUL1 * d, MUL0 + MUL1 * (d + 1))
            weight_loads += [(wnode[at, 0, at], wl1), (wnode[at, 1, at], wsi1)]
        for d in range(3):
            at = slice(MUL0 + MUL1 * d, MUL0 + MUL1 * (d + 1))
            weight_loads += [(w_out[MUL0:P, d, at], w01), (w_out[MUL1 * d:MUL1 * (d + 1), 3, at], w11)]
        ALL_W = 16 * len(weight_loads)

        def by_path(eng, windowed, general):
            eng.wait_ge(flag_set, 1)
            outside = eng.value_load(flag_i[0:1, 0:1], min_val=0, max_val=2 * P)
            with eng.If(outside):
                general()
            with eng.Else():
                windowed()

        block = ctx.enter_context(nc.Block())

        @block.sync
        def _(sp):
            sp.dma_start(dst_i[:, :], dst).then_inc(ld_dst, 16)
            sp.dma_start(a_sb[:, :], avec).then_inc(ld_a, 16)
            def load_x(c, first):
                if not first:
                    sp.wait_ge(ld_x, 16 * c)
                    sp.sem_inc(sp_passed, 1)
                at = bass.ds(c * CHUNK, CHUNK)
                sp.dma_start(xres[:, at, :], x_v[:, at, :]).then_inc(ld_x, 16)

            load_x(0, True)
            with sp.Fori(1, CHUNKS) as c:
                load_x(c, False)

            def store_table(c, first):
                sp.wait_ge(l_done, CHUNK * c + CHUNK)
                sp.sem_inc(sp_passed, 1)
                if not first:
                    sp.wait_ge(table_out, 16 * c)
                sp.dma_start(table_v[:, bass.ds(c * CHUNK, CHUNK), :], l_st[:, :, :]).then_inc(table_out, 16)

            store_table(0, True)
            with sp.Fori(1, CHUNKS) as c:
                store_table(c, False)

            def load_half(i, c, first):
                k = i * 2 + c
                if not first:
                    sp.wait_ge(fc1_done, (k - 1) * HALF)
                    sp.sem_inc(sp_passed, 1)
                sp.dma_start(rad[:, c, :], radial[:, bass.ds(k * HALF * GE, HALF * GE)]).then_inc(ld_rad[c], 16)
                if not first:
                    for j in range(HALF * c, HALF * c + HALF):
                        sp.wait_ge(gathered[j], i * (16 * T))
                    sp.sem_inc(sp_passed, 1)
                sp.dma_start(idx[:, c, :], src[:, bass.ds(k * HALF * T, HALF * T)]).then_inc(ld_idx[c], 16)
                if not first:
                    sp.wait_ge(msg_done, (k - 1) * HALF * 4)
                    sp.sem_inc(sp_passed, 1)
                sp.dma_start(attr_sb[:, c, :, :], attr[:, bass.ds(k * HALF * T, HALF * T), :]).then_inc(ld_attr[c], 16)

            def windowed():
                for c in range(2):
                    load_half(0, c, True)
                with sp.Fori(1, TURNS) as i:
                    for c in range(2):
                        load_half(i, c, False)

            def general():
                sp.wait_ge(zeroed, 3)
                with sp.Fori(0, ND // P) as b:
                    sp.dma_start(sums_d[bass.ds(b * P, P), :], acc[:, 0, 0:4 * P]).then_inc(g_zeroed, 16)
                with sp.Fori(0, GROUPS) as g:
                    sp.wait_ge(g_free, g + 1)
                    sp.sem_inc(sp_passed, 1)
                    sp.dma_start(rad[:, 0, 0:GE], radial[:, bass.ds(g * GE, GE)]).then_inc(g_loaded, 16)
                    sp.dma_start(idx[:, 0, 0:T], src[:, bass.ds(g * T, T)]).then_inc(g_loaded, 16)
                    sp.dma_start(attr_sb[:, 0, 0:T, :], attr[:, bass.ds(g * T, T), :]).then_inc(g_loaded, 16)
                sp.wait_ge(g_turn, TILES + 1)
                with sp.Fori(0, BLOCKS) as b:
                    sp.wait_ge(g_block_free, b + 1)
                    sp.sem_inc(sp_passed, 1)
                    sp.dma_start(rows_in, sums_d[bass.ds(b * P, P), :]).then_inc(g_block_in, 16)

            by_path(sp, windowed, general)

            with sp.Fori(0, CHUNKS) as c:
                sp.wait_ge(fin_done, c * CHUNK + CHUNK)
                sp.sem_inc(sp_passed, 1)
                at = bass.ds(c * CHUNK, CHUNK)
                sp.dma_start(out_v[:, at, :], xres[:, at, :]).then_inc(stored, 16)
            sp.wait_ge(stored, 16 * CHUNKS)

        @block.gpsimd
        def _(pool):
            nc.gpsimd.memset(wnode[:, :, :], 0.0).then_inc(zeroed, 1)
            nc.gpsimd.memset(w_out[:, :, :], 0.0).then_inc(zeroed, 1)
            nc.gpsimd.memset(ident[:, :], 0.0).then_inc(consts, 1)
            nc.gpsimd.memset(ones[:, :], 1.0).then_inc(consts, 1)
            nc.gpsimd.memset(eps[:, :], EPS).then_inc(consts, 1)
            nc.gpsimd.iota(iota_i[:, :], pattern=[[1, W]], base=0, channel_multiplier=0).then_inc(consts, 1)
            pool.wait_ge(consts, 4)
            nc.gpsimd.affine_select(out=ident[:, :], in_=ident[:, :], compare_op=ALU.not_equal, fill=1.0, base=0,
                                    pattern=[[-1, P]], channel_multiplier=1).then_inc(consts, 1)
            nc.gpsimd.tensor_copy(iota_w[:, :], iota_i[:, :]).then_inc(consts, 1)
            nc.gpsimd.affine_select(out=lower[:, :], in_=ones[:, :], compare_op=ALU.is_gt, fill=0.0, base=0,
                                    pattern=[[-1, P]], channel_multiplier=1).then_inc(consts, 1)
            nc.gpsimd.iota(trash_i[:, :], pattern=[[1, 1]], base=TRASH, channel_multiplier=1).then_inc(consts, 1)
            pool.wait_ge(consts, 8)
            nc.gpsimd.tensor_copy(trash[:, :], trash_i[:, :]).then_inc(consts, 1)
            nc.gpsimd.memset(acc[:, :, :], 0.0).then_inc(zeroed, 1)
            pool.wait_ge(table_out, 16 * CHUNKS)

            def gather_group(i, j, first):
                if j % HALF == 0:
                    pool.wait_ge(ld_idx[j // HALF], i * 16 + 16)
                if not first:
                    pool.wait_ge(msg_done, (i * G + j - G + 1) * 4)
                    pool.sem_inc(pool_passed, 1)
                for t in range(T):
                    col = (j % HALF) * T + t
                    nc.gpsimd.indirect_dma_start(
                        out=y[:, j, t, :], out_offset=None, in_=table,
                        in_offset=bass.IndirectOffsetOnAxis(ap=idx[:, j // HALF, col:col + 1], axis=0),
                    ).then_inc(gathered[j], 16)

            def windowed():
                for j in range(G):
                    gather_group(0, j, True)
                with pool.Fori(1, TURNS) as i:
                    for j in range(G):
                        gather_group(i, j, False)

            def general():
                pool.wait_ge(g_zeroed, 16 * (ND // P))
                pool.sem_inc(g_turn, 1)
                with pool.Fori(0, GROUPS) as g:
                    pool.wait_ge(g_loaded, g * 48 + 48)
                    pool.sem_inc(pool_passed, 1)
                    for t in range(T):
                        nc.gpsimd.indirect_dma_start(
                            out=y[:, 0, t, :], out_offset=None, in_=table,
                            in_offset=bass.IndirectOffsetOnAxis(ap=idx[:, 0, t:t + 1], axis=0),
                        ).then_inc(g_rows, 16)
                    for t in range(T):
                        n = g * T + t
                        pool.wait_ge(g_taken, n + 1)
                        pool.sem_inc(pool_passed, 1)
                        nc.gpsimd.indirect_dma_start(
                            out=sums_d, out_offset=bass.IndirectOffsetOnAxis(ap=idx_sum[:, :], axis=0),
                            in_=sums, in_offset=None, compute_op=ALU.add,
                        ).then_inc(g_added, 16)
                        pool.wait_ge(g_added, n * 16 + 16)
                        pool.sem_inc(g_turn, 1)

            by_path(pool, windowed, general)

        @block.scalar
        def _(act):
            act.wait_ge(zeroed, 2)
            for to, frm in weight_loads:
                act.dma_start(to, frm).then_inc(ld_w, 16)
            act.wait_ge(consts, 3)

            def chunk(c, first):
                act.wait_ge(aggr_done, c + 1)
                nc.scalar.activation(std[:, :], mean_var[:, :, 1], ACT.Sqrt, bias=eps[:, :], scale=1.0).then_inc(std_done, 1)
                act.wait_ge(norm_done, c + 1)

                def move(b):
                    act.wait_ge(tr_done, c * CHUNK + b + 1)
                    nc.scalar.activation(hid_t[:, b, 0, :], ps_h[:, b % 2, 0:P], ACT.Copy).then_inc(hidt_a, 1)

                for b in range(CHUNK):
                    if not first:
                        act.wait_ge(tr_done, (c - 1) * CHUNK + b + 1)
                    nc.scalar.activation(hid[:, b, :], xres[:, bass.ds(c * CHUNK + b, 1), :], ACT.Relu,
                                         bias=shift[:, b:b + 1], scale=rstd[:, b:b + 1]).then_inc(hid_done, 1)
                    if b >= 1:
                        move(b - 1)
                move(CHUNK - 1)

            chunk(0, True)
            with act.Fori(1, CHUNKS) as c:
                chunk(c, False)

            def relu(g, s, first):
                act.wait_ge(fc1_done, g + 1)
                if not first:
                    act.wait_ge(fc2_done, g - 1)
                nc.scalar.activation(hr[:, s, :], ps_h[0:N_RADIAL, s, 0:GE], ACT.Relu, scale=K_RADIAL).then_inc(relu_done, 1)

            def windowed():
                for j in range(G):
                    relu(j, j % 2, j < 2)
                with act.Fori(1, TURNS) as i:
                    for j in range(G):
                        relu(i * G + j, j % 2, False)

            def general():
                with act.Fori(0, GROUPS) as g:
                    act.wait_ge(g_fc1, g + 1)
                    nc.scalar.activation(hr[:, 0, :], ps_h[0:N_RADIAL, 0, 0:GE], ACT.Relu, scale=K_RADIAL).then_inc(g_relu, 1)

            by_path(act, windowed, general)

            act.wait_ge(path_done, 1)

            def copy_block(b, s, first):
                if not first:
                    act.wait_ge(fin_mm, b - 1)
                nc.scalar.activation(fin_in[:, s, :].rearrange("p (v n) -> p v n", v=4), acc[:, :, bass.ds(b * P, P)],
                                     ACT.Copy).then_inc(fin_copied, 1)

            for s in range(2):
                copy_block(s, s, True)
            with act.Fori(1, BLOCKS // 2) as b2:
                for s in range(2):
                    copy_block(b2 * 2 + s, s, False)
            copy_block(BLOCKS - 1, 0, False)

        @block.vector
        def _(dve):
            dve.wait_ge(ld_dst, 16)
            nc.vector.tensor_copy(dst_rel[:, :], dst_i[:, :]).then_inc(dst_step, 1)
            nc.vector.tensor_copy(base_i[:, :], dst_i[0:1, 0:TILES:T])
            nc.vector.tensor_copy(base_f[:, :], dst_i[0:1, 0:TILES:T]).then_inc(dst_step, 1)
            dve.wait_ge(base_bc, 1)
            dve.wait_ge(dst_step, 2)
            by_group = dst_rel[:, :].rearrange("p (g t) -> p g t", t=T)
            nc.vector.tensor_tensor(by_group, by_group, ps_s[:, 0, 0:GROUPS].unsqueeze(2).to_broadcast([P, GROUPS, T]),
                                    ALU.subtract).then_inc(dst_step, 1)
            dve.wait_ge(dst_step, 3)
            nc.vector.tensor_reduce(span[:, 0:1], dst_rel[:, :], AX.X, ALU.max).then_inc(dst_step, 1)
            nc.vector.tensor_reduce(span[:, 1:2], dst_rel[:, :], AX.X, ALU.min).then_inc(dst_step, 1)
            dve.wait_ge(dst_step, 5)
            nc.vector.tensor_scalar(span[:, 2:3], span[:, 0:1], float(W) - 0.5, None, ALU.is_gt).then_inc(dst_step, 1)
            nc.vector.tensor_scalar(span[:, 3:4], span[:, 1:2], -0.5, None, ALU.is_lt).then_inc(dst_step, 1)
            dve.wait_ge(flag_sum, 1)
            nc.vector.tensor_copy(flag_i[:, :], ps_s[0:1, 1, 0:1]).then_inc(flag_set, 1)

            dve.wait_ge(ld_w, ALL_W)
            for tile, scale in ((wnode[:, :, 0:MUL0], MUL0 ** -0.5), (wnode[:, :, MUL0:P], MUL1 ** -0.5),
                                (wnode_z[:, :, :], MUL1 ** -0.5), (w_out[0:3 * MUL1, 3, :], K_SUM),
                                (w_out[:, 0:3, :], K_SUM), (w_out[3 * MUL1:P, 3, :], K_SUM * K_DOT)):
                nc.vector.tensor_scalar(tile, tile, float(scale), None, ALU.mult).then_inc(w_scaled, 1)

            dve.wait_ge(ld_a, 16)

            def chunk(c, first):
                dve.wait_ge(ld_x, c * 16 + 16)
                for b in range(CHUNK):
                    nc.vector.bn_stats(stats[:, b, :], xres[:, bass.ds(c * CHUNK + b, 1), :].rearrange("p b c -> p (b c)")).then_inc(bn_done, 1)
                dve.wait_ge(bn_done, c * CHUNK + CHUNK)
                dve.sem_inc(dve_passed, 1)
                for b in range(CHUNK):
                    ins = nc.vector.bn_aggr(mean_var[:, b, :], stats[:, b, :])
                    if b == CHUNK - 1:
                        ins.then_inc(aggr_done, 1)
                dve.wait_ge(std_done, c + 1)
                if not first:
                    dve.wait_ge(hid_done, c * CHUNK)
                nc.vector.reciprocal(rstd[:, :], std[:, :]).then_inc(rstd_done, 1)
                dve.wait_ge(rstd_done, c + 1)
                nc.vector.scalar_tensor_tensor(shift[:, :], mean_var[:, :, 0], -1.0, rstd[:, :], ALU.mult, ALU.mult).then_inc(norm_done, 1)

                def move(b):
                    dve.wait_ge(tr_done, c * CHUNK + b + 1)
                    nc.vector.tensor_copy(hid_t[0:MUL1, b, 1, :], ps_s[0:MUL1, b % 2, 0:P]).then_inc(hidt_b, 1)

                def take(b):
                    dve.wait_ge(node_mm, c * CHUNK + b + 1)
                    if not first and b == 0:
                        dve.wait_ge(table_out, c * 16)
                    pair = ps_w[:, b % 2, 0:2, :]
                    nc.vector.tensor_scalar(l_st[:, b, :], pair[:, 0, 0:C], a_sb[:, bass.ds(c * CHUNK + b, 1)], None, ALU.mult).then_inc(l_done, 1)
                    xr = xres[:, bass.ds(c * CHUNK + b, 1), :].rearrange("p b c -> p (b c)")
                    nc.vector.scalar_tensor_tensor(xr, pair[:, 1, 0:C], a_sb[:, bass.ds(c * CHUNK + b, 1)], xr,
                                                   ALU.mult, ALU.add).then_inc(res_done, 1)

                for b in range(CHUNK):
                    move(b)
                    if b >= 1:
                        take(b - 1)
                take(CHUNK - 1)

            chunk(0, True)
            with dve.Fori(1, CHUNKS) as c:
                chunk(c, False)
            dve.wait_ge(consts, 9)
            dve.wait_ge(zeroed, 3)

            def attr_of(j, a, b):
                return attr_sb[:, j // HALF, (j % HALF) * T:(j % HALF) * T + T, a:b]

            def edge_dots(j):
                nc.vector.tensor_tensor(dots[:, :, :, :], vectors(j), attr_of(j, 1, 4).unsqueeze(3).to_broadcast([P, T, 3, MUL1]),
                                        ALU.mult).then_inc(dots_done, 1)

            def sum_dots():
                nc.vector.tensor_reduce(dot[:, :, :], dots[:, :, :, :].rearrange("p t d u -> p t u d"), AX.X, ALU.add).then_inc(dot_done, 1)

            def vectors(j):
                return y[:, j, :, MUL0:C].rearrange("p t (d u) -> p t d u", d=3)

            def scalar_products(j, s):
                nc.vector.tensor_tensor(msg[:, s, :, 0:2 * MUL0].rearrange("p t (k u) -> p t k u", k=2),
                                        ps_w[:, s, :, 0:2 * MUL0].rearrange("p t (k u) -> p t k u", k=2),
                                        y[:, j, :, 0:MUL0].unsqueeze(2).to_broadcast([P, T, 2, MUL0]), ALU.mult).then_inc(msg_done, 1)

            def vector_products(j, s):
                nc.vector.tensor_tensor(msg[:, s, :, 2 * MUL0:M - MUL1].rearrange("p t (d u) -> p t d u", d=3),
                                        ps_w[:, s, :, 2 * MUL0:NW - MUL1].unsqueeze(2).to_broadcast([P, T, 3, MUL1]),
                                        vectors(j), ALU.mult).then_inc(msg_done, 1)

            def dot_products(s):
                nc.vector.tensor_tensor(msg[:, s, :, M - MUL1:M], ps_w[:, s, :, NW - MUL1:NW], dot[:, :, :], ALU.mult).then_inc(msg_done, 1)

            def messages(i, j):
                g, s = i * G + j, j % 2
                if j % HALF == 0:
                    dve.wait_ge(ld_attr[j // HALF], i * 16 + 16)
                nc.vector.tensor_tensor(hot[:, s, :, 0, :], iota_w[:, :].unsqueeze(1).to_broadcast([P, T, W]),
                                        dst_rel[:, bass.ds(g * T, T)].unsqueeze(2).to_broadcast([P, T, W]),
                                        ALU.is_equal).then_inc(hot_done, 1)
                dve.wait_ge(gathered[j], i * (16 * T) + 16 * T)
                edge_dots(j)
                dve.wait_ge(hot_done, g + 1)
                nc.vector.tensor_tensor(hot[:, s, :, 1:V, :], hot[:, s, :, 0:1, :].to_broadcast([P, T, 4, W]),
                                        attr_of(j, 0, 4).unsqueeze(3).to_broadcast([P, T, 4, W]), ALU.mult).then_inc(msg_done, 1)
                dve.wait_ge(dots_done, g + 1)
                sum_dots()
                dve.wait_ge(fc2_done, g + 1)
                scalar_products(j, s)
                vector_products(j, s)
                dve.wait_ge(dot_done, g + 1)
                dot_products(s)

            def accumulate(g, s, base, first):
                dve.wait_ge(win_done, g + 1)
                if not first:
                    dve.wait_ge(acc_done, g * 4)
                p = ps_s[:, s, :]
                for rows, slots, cols in ((slice(0, MUL0), slice(0, 1), slice(0, W)),
                                          (slice(MUL0, P), slice(0, 3), slice(W, 4 * W)),
                                          (slice(0, 3 * MUL1), slice(3, 4), slice(5 * W, 6 * W)),
                                          (slice(3 * MUL1, P), slice(3, 4), slice(4 * W, 5 * W))):
                    to = acc[rows, slots, bass.ds(base, W)]
                    nc.vector.tensor_tensor(to, to, p[rows, cols].rearrange("p (v n) -> p v n", n=W), ALU.add).then_inc(acc_done, 1)

            def base_of(g):
                return dve.value_load(base_i[0:1, bass.ds(g, 1)], min_val=0, max_val=N - 1)

            def windowed():
                for j in range(G):
                    messages(0, j)
                    if j > 0:
                        accumulate(j - 1, (j - 1) % 2, base_of(j - 1), j == 1)
                with dve.Fori(1, TURNS) as i:
                    for j in range(G):
                        messages(i, j)
                        accumulate(i * G + j - 1, (j - 1) % 2, base_of(i * G + j - 1), False)
                accumulate(GROUPS - 1, (GROUPS - 1) % 2, base_of(GROUPS - 1), False)
                dve.wait_ge(acc_done, 4 * GROUPS)
                dve.sem_inc(path_done, 1)

            def general():
                nc.vector.memset(full, 0.0)
                dve.sem_inc(g_free, 1)
                with dve.Fori(0, GROUPS) as g:
                    dve.wait_ge(g_loaded, g * 48 + 48)
                    dve.wait_ge(g_rows, g * (16 * T) + 16 * T)
                    edge_dots(0)
                    dve.drain()
                    sum_dots()
                    dve.wait_ge(g_fc2, g + 1)
                    scalar_products(0, 0)
                    vector_products(0, 0)
                    dve.drain()
                    dot_products(0)
                    for t in range(T):
                        n = g * T + t
                        nc.vector.tensor_copy(dst_col[:, :], dst_i[:, bass.ds(n, 1)])
                        dve.drain()
                        nc.vector.tensor_copy(dst_bc, dst_col[:, :].to_broadcast([P, P])).then_inc(g_col, 1)
                        dve.drain()
                        part = msg[:, 0, t, :]
                        for at, frm, k in ((0, slice(0, MUL0), 0), (MUL0, slice(MUL0, 2 * MUL0), 1),
                                           (P + MUL0, slice(MUL0, 2 * MUL0), 2), (2 * P + MUL0, slice(MUL0, 2 * MUL0), 3),
                                           (3 * P, slice(2 * MUL0, M - MUL1), 0)):
                            nc.vector.tensor_scalar(full[:, at:at + frm.stop - frm.start], part[:, frm],
                                                    attr_sb[:, 0, t, k:k + 1], None, ALU.mult)
                        nc.vector.tensor_copy(full[:, 4 * P - MUL1:4 * P], part[:, M - MUL1:M])
                        dve.wait_ge(g_turned, n + 1)
                        nc.vector.tensor_tensor(same, ps_s[:, 0, 0:P], dst_col[:, :].to_broadcast([P, P]), ALU.is_equal)
                        dve.drain()
                        dve.sem_inc(g_full, 1)
                        nc.vector.tensor_tensor(same_before, same, lower[:, :], ALU.mult)
                        nc.vector.tensor_tensor(away[:, :], trash[:, :], dst_col[:, :], ALU.subtract)
                        dve.drain()
                        nc.vector.tensor_reduce(repeats[:, :], same_before, AX.X, ALU.max)
                        dve.drain()
                        nc.vector.tensor_tensor(away[:, :], away[:, :], repeats[:, :], ALU.mult)
                        dve.drain()
                        dve.wait_ge(g_turn, n + 1)
                        nc.vector.tensor_tensor(idx_sum[:, :], away[:, :], dst_col[:, :], ALU.add)
                        dve.wait_ge(g_summed, n + 1)
                        nc.vector.tensor_copy(sums, ps_s[:, 1, :])
                        dve.drain()
                        dve.sem_inc(g_taken, 1)
                    dve.sem_inc(g_free, 1)
                dve.sem_inc(g_block_free, 1)
                with dve.Fori(0, BLOCKS) as b:
                    dve.wait_ge(g_block_turned, b + 1)
                    nc.vector.tensor_copy(acc[:, :, bass.ds(b * P, P)], ps_w[:, 0, :, 0:P]).then_inc(g_block_free, 1)
                dve.drain()
                dve.sem_inc(path_done, 1)

            by_path(dve, windowed, general)

            def finish(b, s):
                dve.wait_ge(fin_mm, b + 1)
                xr = xres[:, bass.ds(b, 1), :].rearrange("p b c -> p (b c)")
                nc.vector.scalar_tensor_tensor(xr, ps_w[:, s, 0, 0:C], a_sb[:, bass.ds(b, 1)], xr, ALU.mult, ALU.add).then_inc(fin_done, 1)

            with dve.Fori(0, BLOCKS // 2) as b2:
                for s in range(2):
                    finish(b2 * 2 + s, s)
            finish(BLOCKS - 1, 0)

        @block.tensor
        def _(pe):
            pe.wait_ge(consts, 9)
            pe.wait_ge(dst_step, 2)
            nc.tensor.matmul(ps_s[:, 0, 0:GROUPS], ones[0:1, :], base_f[:, :], start=True, stop=True).then_inc(base_bc, 1)
            pe.wait_ge(dst_step, 7)
            nc.tensor.matmul(ps_s[0:1, 1, 0:1], ones[:, 0:1], span[:, 2:3], start=True, stop=False)
            nc.tensor.matmul(ps_s[0:1, 1, 0:1], ones[:, 0:1], span[:, 3:4], start=False, stop=True).then_inc(flag_sum, 1)
            pe.wait_ge(w_scaled, 6)
            pe.wait_ge(flag_set, 1)

            def had_bank(b):
                return b - 2 if b >= 2 else -1 - b

            def chunk(c, first):
                def turn_block(b):
                    pe.wait_ge(hid_done, c * CHUNK + b + 1)
                    if b >= 2 or not first:
                        before = c * CHUNK + had_bank(b)
                        pe.wait_ge(hidt_a, before + 1)
                        pe.wait_ge(hidt_b, before + 1)
                    nc.tensor.transpose(ps_h[:, b % 2, 0:P], hid[:, b, 0:P], ident[:, :])
                    nc.tensor.transpose(ps_s[0:MUL1, b % 2, 0:P], hid[:, b, P:C], ident[:, :]).then_inc(tr_done, 1)

                def linear(b):
                    pe.wait_ge(hidt_a, c * CHUNK + b + 1)
                    pe.wait_ge(hidt_b, c * CHUNK + b + 1)
                    if b >= 2 or not first:
                        before = c * CHUNK + had_bank(b)
                        pe.wait_ge(l_done, before + 1)
                        pe.wait_ge(res_done, before + 1)
                    pair = ps_w[:, b % 2, 0:2, :]
                    nc.tensor.matmul(pair[:, :, 0:P], hid_t[:, b, 0, :], wnode[:, :, :], start=True, stop=True)
                    nc.tensor.matmul(pair[:, :, P:C], hid_t[0:MUL1, b, 1, :], wnode_z[:, :, :], start=True, stop=True).then_inc(node_mm, 1)

                for b in range(CHUNK):
                    turn_block(b)
                    if b >= 1:
                        linear(b - 1)
                linear(CHUNK - 1)

            chunk(0, True)
            with pe.Fori(1, CHUNKS) as c:
                chunk(c, False)

            def fc1(i, j):
                if j % HALF == 0:
                    pe.wait_ge(ld_rad[j // HALF], i * 16 + 16)
                nc.tensor.matmul(ps_h[0:N_RADIAL, j % 2, 0:GE], w_fc1[:, :], rad[:, j // HALF, (j % HALF) * GE:(j % HALF + 1) * GE],
                                 start=True, stop=True).then_inc(fc1_done, 1)

            def fc2(g, s):
                pe.wait_ge(relu_done, g + 1)
                for t in range(T):
                    ins = nc.tensor.matmul(ps_w[:, s, t, 0:NW], hr[:, s, t * P:(t + 1) * P], w_fc2[:, :], start=True, stop=True)
                ins.then_inc(fc2_done, 1)

            def windows(g, s, first):
                pe.wait_ge(msg_done, g * 4 + 4)
                if not first:
                    pe.wait_ge(acc_done, (g - 1) * 4)
                for t in range(T):
                    nc.tensor.matmul(ps_s[:, s, 0:4 * W], msg[:, s, t, 0:P], hot[:, s, t, 1:V, :], start=(t == 0), stop=(t == T - 1))
                for t in range(T):
                    ins = nc.tensor.matmul(ps_s[:, s, 4 * W:6 * W], msg[:, s, t, P:M], hot[:, s, t, 0:2, :], start=(t == 0), stop=(t == T - 1))
                ins.then_inc(win_done, 1)

            def node_stage_left():
                pe.wait_ge(l_done, BLOCKS)
                pe.wait_ge(res_done, BLOCKS)

            def windowed():
                for j in range(G):
                    fc1(0, j)
                    if j == 1:
                        node_stage_left()
                    if j >= 1:
                        fc2(j - 1, (j - 1) % 2)
                    if j >= 2:
                        windows(j - 2, j % 2, j < 4)
                with pe.Fori(1, TURNS) as i:
                    for j in range(G):
                        g = i * G + j
                        fc1(i, j)
                        fc2(g - 1, (j - 1) % 2)
                        windows(g - 2, j % 2, False)
                fc2(GROUPS - 1, (GROUPS - 1) % 2)
                windows(GROUPS - 2, 0, False)
                windows(GROUPS - 1, 1, False)

            def general():
                node_stage_left()
                with pe.Fori(0, GROUPS) as g:
                    pe.wait_ge(g_loaded, g * 48 + 48)
                    nc.tensor.matmul(ps_h[0:N_RADIAL, 0, 0:GE], w_fc1[:, :], rad[:, 0, 0:GE], start=True, stop=True).then_inc(g_fc1, 1)
                    pe.wait_ge(g_relu, g + 1)
                    for t in range(T):
                        ins = nc.tensor.matmul(ps_w[:, 0, t, 0:NW], hr[:, 0, t * P:(t + 1) * P], w_fc2[:, :], start=True, stop=True)
                    ins.then_inc(g_fc2, 1)
                    for t in range(T):
                        n = g * T + t
                        pe.wait_ge(g_col, n + 1)
                        nc.tensor.transpose(ps_s[:, 0, 0:P], dst_bc, ident[:, :]).then_inc(g_turned, 1)
                        pe.wait_ge(g_full, n + 1)
                        nc.tensor.matmul(ps_s[:, 1, :], same, full, start=True, stop=True).then_inc(g_summed, 1)
                with pe.Fori(0, BLOCKS) as b:
                    pe.wait_ge(g_block_in, b * 16 + 16)
                    for v in range(4):
                        ins = nc.tensor.transpose(ps_w[:, 0, v, 0:P], rows_in[:, v * P:(v + 1) * P], ident[:, :])
                    ins.then_inc(g_block_turned, 1)

            by_path(pe, windowed, general)

            def last_linear(b, s, first):
                pe.wait_ge(fin_copied, b + 1)
                if not first:
                    pe.wait_ge(fin_done, b - 1)
                o = ps_w[:, s, 0, :]
                a = fin_in[:, s, :]
                nc.tensor.matmul(o[:, 0:C], a[:, 3 * P:4 * P], w_out[:, 3, :], start=True, stop=False)
                nc.tensor.matmul(o[:, 0:MUL0 + MUL1], a[:, 0:P], w_out[:, 0, 0:MUL0 + MUL1], start=False, stop=False)
                for d in (1, 2):
                    at = slice(MUL0 + MUL1 * d, MUL0 + MUL1 * (d + 1))
                    ins = nc.tensor.matmul(o[:, at], a[:, d * P:(d + 1) * P], w_out[:, d, at], start=False, stop=(d == 2))
                ins.then_inc(fin_mm, 1)

            for s in range(2):
                last_linear(s, s, True)
            with pe.Fori(1, BLOCKS // 2) as b2:
                for s in range(2):
                    last_linear(b2 * 2 + s, s, False)
            last_linear(BLOCKS - 1, 0, False)


ORDER = np.concatenate([np.arange(MUL0)] + [MUL0 + 3 * np.arange(MUL1) + d for d in range(3)])


def kernel(**inputs):
    import concourse.bacc as bacc
    from concourse.bass_utils import run_bass_kernel_spmd

    get = {k: np.asarray(v) for k, v in inputs.items()}

    def by_tile(v, fill):
        padded = np.concatenate([v, np.broadcast_to(fill, (EP - E, *v.shape[1:])).astype(v.dtype)])
        return np.ascontiguousarray(np.moveaxis(padded.reshape(TILES, P, *v.shape[1:]), 0, 1))

    def padded_rows(v):
        return np.concatenate([v, np.zeros((NP - N, v.shape[1]), v.dtype)])

    radial = np.zeros((N_BASIS, EP), np.float32)
    radial[:, :E] = get["edge_attr_10"].T
    arrays = {
        "x": np.ascontiguousarray(padded_rows(get["x"])[:, ORDER]),
        "src": by_tile(get["src"], 0),
        "dst": by_tile(get["dst"], get["dst"][-1]),
        "radial": radial,
        "attr": by_tile(get["edge_attr_4"], 0),
        "avec": np.ascontiguousarray(padded_rows(get["node_vec1"]).reshape(BLOCKS, P).T),
    }
    for k in ("W_si0", "W_si1", "W_l1_0", "W_l1_1", "W_l2_00", "W_l2_10", "W_l2_01", "W_l2_11", "W_fc1", "W_fc2"):
        arrays[k] = np.ascontiguousarray(get["L0_gnn_" + k])
    nc = bacc.Bacc("TRN2", target_bir_lowering=False, num_devices=1)
    args = [nc.dram_tensor(f"in_{k}", a.shape, mybir.dt.from_np(a.dtype), kind="ExternalInput").ap() for k, a in arrays.items()]
    args.append(nc.dram_tensor("out", (NP, C), F32, kind="ExternalOutput").ap())
    gnn_layer(nc, *args)
    r = run_bass_kernel_spmd(nc, [{f"in_{k}": a for k, a in arrays.items()}], core_ids=[0])
    rows = np.asarray(r.results[0]["out"])[:N]
    result = np.empty_like(rows)
    result[:, ORDER] = rows
    return result
```

```python
import numpy as np
import concourse.bass as bass
from concourse import mybir
from contextlib import ExitStack

P = 128
N = 6250
E = 206250
MUL0, MUL1 = 64, 32
C = MUL0 + 3 * MUL1
N_BASIS, N_RADIAL = 10, 100
NW = 2 * MUL0 + 2 * MUL1
BLOCKS = -(-N // P)
CHUNK = 7
CHUNKS = BLOCKS // CHUNK
assert CHUNKS * CHUNK == BLOCKS
NP = BLOCKS * P

T = 4
W = 32
V = 5
G = 4
HALF = 2
TURNS = -(-E // (P * T * G))
GROUPS = TURNS * G
TILES = GROUPS * T
PAIRS = TURNS // 2
assert TURNS == 2 * PAIRS + 1
LAG = 3
IN_LOOP = PAIRS - LAG
FIN = 6 * W
EP = TILES * P
GE = T * P
NA = N + W
M = 2 * P
TRASH = NP
ND = NP + P

EPS = 1e-5
K_RADIAL = float(np.sqrt(2.0) / np.sqrt(N_BASIS))
K_SUM = float(0.5 / np.sqrt(16.0) / np.sqrt(MUL0 + MUL1) / np.sqrt(N_RADIAL))
K_DOT = float(1.0 / np.sqrt(3.0))

F32 = mybir.dt.float32
I32 = mybir.dt.int32
ALU = mybir.AluOpType
ACT = mybir.ActivationFunctionType
AX = mybir.AxisListType


def gnn_layer(nc, x, src, dst, radial, attr, avec, w_node, w_node_z, w_last, wf1, wf2, out):
    ctx = ExitStack()
    with ctx:
        def sb(name, shape, dt=F32):
            return ctx.enter_context(nc.sbuf_tensor(name, shape, dt))

        def sem(name):
            return ctx.enter_context(nc.semaphore(name))

        table = nc.dram_tensor("table", (NP, C), F32).ap()
        sums_d = nc.dram_tensor("sums_d", (ND, 4 * P), F32).ap()

        acc = sb("acc", [P, 4, NA])
        xres = sb("xres", [P, BLOCKS, C])
        a_sb = sb("a_sb", [P, BLOCKS])
        dst_i = sb("dst_i", [P, TILES], I32)
        dst_rel = sb("dst_rel", [P, TILES])
        base_f = sb("base_f", [1, GROUPS])
        base_i = sb("base_i", [1, GROUPS], I32)
        iota_i = sb("iota_i", [P, W], I32)
        iota_w = sb("iota_w", [P, W])
        ident = sb("ident", [P, P])
        ones = sb("ones", [P, P])
        span = sb("span", [P, 6])
        flag_i = sb("flag_i", [1, 1], I32)
        wnode = sb("wnode", [P, 2, P])
        wnode_z = sb("wnode_z", [MUL1, 2, MUL1])
        w_fc1 = sb("w_fc1", [N_BASIS, N_RADIAL])
        w_fc2 = sb("w_fc2", [N_RADIAL, NW])
        w_out = sb("w_out", [P, 4, C])
        stats = sb("stats", [P, CHUNK, 6])
        mean_var = sb("mean_var", [P, CHUNK, 2])
        eps = sb("eps", [P, 1])
        std = sb("std", [P, CHUNK])
        rstd = sb("rstd", [P, BLOCKS])
        shift = sb("shift", [P, BLOCKS])
        hid = sb("hid", [P, CHUNK, C])
        hid_t = sb("hid_t", [P, CHUNK, 2, P])
        l_st = sb("l_st", [P, CHUNK, C])
        idx = sb("idx", [P, 2, HALF * T], I32)
        attr_sb = sb("attr_sb", [P, 2, HALF * T, 4])
        rad = sb("rad", [N_BASIS, 2, HALF * GE])
        y = sb("y", [P, G, T, C])
        hr = sb("hr", [N_RADIAL, 2, GE])
        msg = sb("msg", [P, 2, T, M])
        hot = sb("hot", [P, 2, T, V, W])
        dots = sb("dots", [P, T, 3, MUL1])
        dot = sb("dot", [P, T, MUL1])
        fin_in = sb("fin_in", [P, 4, P])
        least = y[:, :, :, :].rearrange("p g t c -> p (g t c)")[:, 0:TILES].bitcast(I32)
        above = msg[:, :, :, :].rearrange("p s t m -> p (s t m)")[:, 0:TILES].bitcast(I32)
        spare = msg[:, 1, :, :].rearrange("p t m -> p (t m)")
        full, sums = spare[:, 0:4 * P], spare[:, 4 * P:8 * P]
        spare = hot[:, 1, :, :, :].rearrange("p t v w -> p (t v w)")
        same, same_before, dst_bc = (spare[:, n * P:(n + 1) * P] for n in range(3))
        lower = sb("lower", [P, P])
        dst_col = sb("dst_col", [P, 1])
        repeats = sb("repeats", [P, 1])
        trash_i = sb("trash_i", [P, 1], I32)
        trash = sb("trash", [P, 1])
        away = sb("away", [P, 1])
        idx_sum = sb("idx_sum", [P, 1], I32)
        rows_in = y[:, 0, :, :].rearrange("p t c -> p (t c)")[:, 0:4 * P]

        def ps(name, shape):
            return ctx.enter_context(nc.psum_tensor(name, shape, F32))

        ps_h = ps("ps_h", [P, 2, 512])
        ps_w = ps("ps_w", [P, 2, T, 256])
        ps_s = ps("ps_s", [P, 2, 512])

        sp_passed, dve_passed, pool_passed = sem("sp_passed"), sem("dve_passed"), sem("pool_passed")
        ld_x = sem("ld_x")
        ld_dst = sem("ld_dst")
        ld_a = sem("ld_a")
        ld_w = sem("ld_w")
        ld_wnode = sem("ld_wnode")
        zeroed = sem("zeroed")
        consts = sem("consts")
        dst_step = sem("dst_step")
        base_bc = sem("base_bc")
        flag_sum = sem("flag_sum")
        flag_set = sem("flag_set")
        order_step = sem("order_step")
        w_scaled = sem("w_scaled")
        bn_done = sem("bn_done")
        aggr_done = sem("aggr_done")
        std_done = sem("std_done")
        rstd_done = sem("rstd_done")
        norm_done = sem("norm_done")
        hid_done = sem("hid_done")
        tr_done = sem("tr_done")
        hidt_done = sem("hidt_done")
        node_mm = sem("node_mm")
        l_done = sem("l_done")
        res_done = sem("res_done")
        table_out = sem("table_out")
        ld_idx = [sem(f"ld_idx{c}") for c in range(2)]
        ld_attr = [sem(f"ld_attr{c}") for c in range(2)]
        ld_rad = [sem(f"ld_rad{c}") for c in range(2)]
        gathered = [sem(f"gathered{j}") for j in range(G)]
        fc1_done = sem("fc1_done")
        relu_done = sem("relu_done")
        fc2_done = sem("fc2_done")
        hot_done = sem("hot_done")
        dots_done = sem("dots_done")
        dot_done = sem("dot_done")
        msg_done = sem("msg_done")
        win_done = sem("win_done")
        acc_done = sem("acc_done")
        g_zeroed, g_free, g_loaded, g_rows, g_fc1, g_relu, g_fc2 = (
            sem("g_" + n) for n in ("zeroed", "free", "loaded", "rows", "fc1", "relu", "fc2"))
        g_col, g_turned, g_full, g_summed, g_taken, g_added, g_turn = (
            sem("g_" + n) for n in ("col", "turned", "full", "summed", "taken", "added", "turn"))
        g_block_free, g_block_in, g_block_turned = (sem("g_block_" + n) for n in ("free", "in", "turned"))
        fin_copied = sem("fin_copied")
        fin_mm = sem("fin_mm")
        fin_done = sem("fin_done")
        stored = sem("stored")

        table_v = table.rearrange("(b p) c -> p b c", p=P)
        x_v = x.rearrange("(b p) c -> p b c", p=P)
        out_v = out.rearrange("(b p) c -> p b c", p=P)

        def by_path(eng, windowed, general):
            eng.wait_ge(flag_set, 1)
            outside = eng.value_load(flag_i[0:1, 0:1], min_val=0, max_val=3 * P)
            with eng.If(outside):
                general()
            with eng.Else():
                windowed()

        block = ctx.enter_context(nc.Block())

        @block.sync
        def _(sp):
            def load_x(c, first):
                if not first:
                    sp.wait_ge(ld_x, 16 * c)
                    sp.sem_inc(sp_passed, 1)
                at = bass.ds(c * CHUNK, CHUNK)
                sp.dma_start(xres[:, at, :], x_v[:, at, :]).then_inc(ld_x, 16)

            load_x(0, True)
            sp.dma_start(dst_i[:, :], dst).then_inc(ld_dst, 16)
            with sp.Fori(1, CHUNKS) as c:
                load_x(c, False)

            def store_table(c, first):
                sp.wait_ge(l_done, CHUNK * c + CHUNK)
                sp.sem_inc(sp_passed, 1)
                if not first:
                    sp.wait_ge(table_out, 16 * c)
                sp.dma_start(table_v[:, bass.ds(c * CHUNK, CHUNK), :], l_st[:, :, :]).then_inc(table_out, 16)

            store_table(0, True)
            with sp.Fori(1, CHUNKS) as c:
                store_table(c, False)

            def load_half(i, c, first):
                k = i * 2 + c
                if not first:
                    sp.wait_ge(fc1_done, (k - 1) * HALF)
                    sp.sem_inc(sp_passed, 1)
                sp.dma_start(rad[:, c, :], radial[:, bass.ds(k * HALF * GE, HALF * GE)]).then_inc(ld_rad[c], 16)
                if not first:
                    for j in range(HALF * c, HALF * c + HALF):
                        sp.wait_ge(gathered[j], i * (16 * T))
                    sp.sem_inc(sp_passed, 1)
                sp.dma_start(idx[:, c, :], src[:, bass.ds(k * HALF * T, HALF * T)]).then_inc(ld_idx[c], 16)
                if not first:
                    sp.wait_ge(msg_done, (k - 1) * HALF * 4)
                    sp.sem_inc(sp_passed, 1)
                sp.dma_start(attr_sb[:, c, :, :], attr[:, bass.ds(k * HALF * T, HALF * T), :]).then_inc(ld_attr[c], 16)

            def windowed():
                for c in range(2):
                    load_half(0, c, True)
                with sp.Fori(1, TURNS) as i:
                    for c in range(2):
                        load_half(i, c, False)

            def general():
                sp.wait_ge(zeroed, 1)
                with sp.Fori(0, ND // P) as b:
                    sp.dma_start(sums_d[bass.ds(b * P, P), :], acc[:, 0, 0:4 * P]).then_inc(g_zeroed, 16)
                with sp.Fori(0, GROUPS) as g:
                    sp.wait_ge(g_free, g + 1)
                    sp.sem_inc(sp_passed, 1)
                    sp.dma_start(rad[:, 0, 0:GE], radial[:, bass.ds(g * GE, GE)]).then_inc(g_loaded, 16)
                    sp.dma_start(idx[:, 0, 0:T], src[:, bass.ds(g * T, T)]).then_inc(g_loaded, 16)
                    sp.dma_start(attr_sb[:, 0, 0:T, :], attr[:, bass.ds(g * T, T), :]).then_inc(g_loaded, 16)
                sp.wait_ge(g_turn, TILES + 1)
                with sp.Fori(0, BLOCKS) as b:
                    sp.wait_ge(g_block_free, b + 1)
                    sp.sem_inc(sp_passed, 1)
                    sp.dma_start(rows_in, sums_d[bass.ds(b * P, P), :]).then_inc(g_block_in, 16)

            by_path(sp, windowed, general)

            with sp.Fori(0, CHUNKS) as c:
                sp.wait_ge(fin_done, c * CHUNK + CHUNK)
                sp.sem_inc(sp_passed, 1)
                at = bass.ds(c * CHUNK, CHUNK)
                sp.dma_start(out_v[:, at, :], xres[:, at, :]).then_inc(stored, 16)
            sp.wait_ge(stored, 16 * CHUNKS)

        @block.gpsimd
        def _(pool):
            nc.gpsimd.memset(ident[:, :], 0.0).then_inc(consts, 1)
            nc.gpsimd.memset(ones[:, :], 1.0).then_inc(consts, 1)
            nc.gpsimd.memset(eps[:, :], EPS).then_inc(consts, 1)
            nc.gpsimd.iota(iota_i[:, :], pattern=[[1, W]], base=0, channel_multiplier=0).then_inc(consts, 1)
            pool.wait_ge(consts, 4)
            nc.gpsimd.affine_select(out=ident[:, :], in_=ident[:, :], compare_op=ALU.not_equal, fill=1.0, base=0,
                                    pattern=[[-1, P]], channel_multiplier=1).then_inc(consts, 1)
            nc.gpsimd.tensor_copy(iota_w[:, :], iota_i[:, :]).then_inc(consts, 1)
            nc.gpsimd.affine_select(out=lower[:, :], in_=ones[:, :], compare_op=ALU.is_gt, fill=0.0, base=0,
                                    pattern=[[-1, P]], channel_multiplier=1).then_inc(consts, 1)
            nc.gpsimd.iota(trash_i[:, :], pattern=[[1, 1]], base=TRASH, channel_multiplier=1).then_inc(consts, 1)
            pool.wait_ge(consts, 8)
            nc.gpsimd.tensor_copy(trash[:, :], trash_i[:, :]).then_inc(consts, 1)
            ramp = PAIRS * 2 * G * T
            nc.gpsimd.iota(least[:, 0:ramp], pattern=[[P, PAIRS], [0, ramp // PAIRS]], base=-P * (LAG - 1),
                           channel_multiplier=0).then_inc(order_step, 1)
            nc.gpsimd.iota(least[:, ramp:TILES], pattern=[[0, TILES - ramp]], base=P * IN_LOOP,
                           channel_multiplier=0).then_inc(order_step, 1)
            pool.wait_ge(order_step, 2)
            pool.wait_ge(ld_dst, 16)
            nc.gpsimd.tensor_tensor(above, dst_i[:, :], least, ALU.subtract).then_inc(order_step, 1)
            nc.gpsimd.memset(acc[:, :, :], 0.0).then_inc(zeroed, 1)
            pool.wait_ge(table_out, 16 * CHUNKS)

            def gather_group(i, j, first):
                if j % HALF == 0:
                    pool.wait_ge(ld_idx[j // HALF], i * 16 + 16)
                if not first:
                    pool.wait_ge(msg_done, (i * G + j - G + 1) * 4)
                    pool.sem_inc(pool_passed, 1)
                for t in range(T):
                    col = (j % HALF) * T + t
                    nc.gpsimd.indirect_dma_start(
                        out=y[:, j, t, :], out_offset=None, in_=table,
                        in_offset=bass.IndirectOffsetOnAxis(ap=idx[:, j // HALF, col:col + 1], axis=0),
                    ).then_inc(gathered[j], 16)

            def windowed():
                for j in range(G):
                    gather_group(0, j, True)
                with pool.Fori(1, TURNS) as i:
                    for j in range(G):
                        gather_group(i, j, False)

            def general():
                pool.wait_ge(g_zeroed, 16 * (ND // P))
                pool.sem_inc(g_turn, 1)
                with pool.Fori(0, GROUPS) as g:
                    pool.wait_ge(g_loaded, g * 48 + 48)
                    pool.sem_inc(pool_passed, 1)
                    for t in range(T):
                        nc.gpsimd.indirect_dma_start(
                            out=y[:, 0, t, :], out_offset=None, in_=table,
                            in_offset=bass.IndirectOffsetOnAxis(ap=idx[:, 0, t:t + 1], axis=0),
                        ).then_inc(g_rows, 16)
                    for t in range(T):
                        n = g * T + t
                        pool.wait_ge(g_taken, n + 1)
                        pool.sem_inc(pool_passed, 1)
                        nc.gpsimd.indirect_dma_start(
                            out=sums_d, out_offset=bass.IndirectOffsetOnAxis(ap=idx_sum[:, :], axis=0),
                            in_=sums, in_offset=None, compute_op=ALU.add,
                        ).then_inc(g_added, 16)
                        pool.wait_ge(g_added, n * 16 + 16)
                        pool.sem_inc(g_turn, 1)

            by_path(pool, windowed, general)

        @block.scalar
        def _(act):
            act.dma_start(wnode[:, :, :], w_node).then_inc(ld_wnode, 16)
            act.dma_start(wnode_z[:, :, :], w_node_z).then_inc(ld_wnode, 16)
            act.dma_start(a_sb[:, :], avec).then_inc(ld_a, 16)
            act.dma_start(w_out[:, :, :], w_last).then_inc(ld_w, 16)
            act.dma_start(w_fc1[:, :], wf1).then_inc(ld_w, 16)
            act.dma_start(w_fc2[:, :], wf2).then_inc(ld_w, 16)
            act.wait_ge(consts, 3)

            def deviation(c):
                act.wait_ge(aggr_done, c + 1)
                nc.scalar.activation(std[:, :], mean_var[:, :, 1], ACT.Sqrt, bias=eps[:, :], scale=1.0).then_inc(std_done, 1)

            def chunk(c, first, last):
                act.wait_ge(norm_done, c + 1)

                def move(b):
                    act.wait_ge(tr_done, c * CHUNK + b + 1)
                    nc.scalar.activation(hid_t[:, b, 0, :], ps_h[:, b % 2, 0:P], ACT.Copy)
                    nc.scalar.activation(hid_t[0:MUL1, b, 1, :], ps_s[0:MUL1, b % 2, 0:P], ACT.Copy).then_inc(hidt_done, 1)

                for b in range(CHUNK):
                    if not first:
                        act.wait_ge(tr_done, (c - 1) * CHUNK + b + 1)
                    at = bass.ds(c * CHUNK + b, 1)
                    nc.scalar.activation(hid[:, b, :], xres[:, at, :].rearrange("p b c -> p (b c)"), ACT.Relu,
                                         bias=shift[:, at], scale=rstd[:, at]).then_inc(hid_done, 1)
                    if b >= 1:
                        move(b - 1)
                    if b == CHUNK - 3 and not last:
                        deviation(c + 1)
                move(CHUNK - 1)

            deviation(0)
            chunk(0, True, False)
            with act.Fori(1, CHUNKS - 1) as c:
                chunk(c, False, False)
            chunk(CHUNKS - 1, False, True)

            def relu(g, s, first):
                act.wait_ge(fc1_done, g + 1)
                if not first:
                    act.wait_ge(fc2_done, g - 1)
                nc.scalar.activation(hr[:, s, :], ps_h[0:N_RADIAL, s, 0:GE], ACT.Relu, scale=K_RADIAL).then_inc(relu_done, 1)

            def copy_block(b):
                nc.scalar.activation(fin_in[:, :, :], acc[:, :, bass.ds(b * P, P)], ACT.Copy).then_inc(fin_copied, 1)

            def windowed():
                def pair(k, first, finish):
                    for j in range(2 * G):
                        relu(k * (2 * G) + j, j % 2, first and j < 2)
                        if finish and j == 3:
                            act.wait_ge(acc_done, k * (8 * G))
                            copy_block(k - LAG)

                pair(0, True, False)
                with act.Fori(1, LAG) as k:
                    pair(k, False, False)
                with act.Fori(LAG, PAIRS) as k:
                    pair(k, False, True)
                for j in range(G):
                    relu((TURNS - 1) * G + j, j % 2, False)
                act.wait_ge(acc_done, 4 * GROUPS)
                for b in range(IN_LOOP, BLOCKS):
                    act.wait_ge(fin_mm, b)
                    copy_block(b)

            def general():
                with act.Fori(0, GROUPS) as g:
                    act.wait_ge(g_fc1, g + 1)
                    nc.scalar.activation(hr[:, 0, :], ps_h[0:N_RADIAL, 0, 0:GE], ACT.Relu, scale=K_RADIAL).then_inc(g_relu, 1)

                act.wait_ge(g_block_free, BLOCKS + 1)
                copy_block(0)
                with act.Fori(1, BLOCKS) as b:
                    act.wait_ge(fin_mm, b)
                    copy_block(b)

            by_path(act, windowed, general)

        @block.vector
        def _(dve):
            def statistics(c, some):
                for b in some:
                    nc.vector.bn_stats(stats[:, b, :], xres[:, bass.ds(c * CHUNK + b, 1), :].rearrange("p b c -> p (b c)")).then_inc(bn_done, 1)

            def aggregate(c):
                dve.wait_ge(bn_done, c * CHUNK + CHUNK)
                dve.sem_inc(dve_passed, 1)
                for b in range(CHUNK):
                    ins = nc.vector.bn_aggr(mean_var[:, b, :], stats[:, b, :])
                ins.then_inc(aggr_done, 1)

            def normalizers(c):
                dve.wait_ge(std_done, c + 1)
                at = bass.ds(c * CHUNK, CHUNK)
                nc.vector.reciprocal(rstd[:, at], std[:, :]).then_inc(rstd_done, 1)
                dve.wait_ge(rstd_done, c + 1)
                nc.vector.scalar_tensor_tensor(shift[:, at], mean_var[:, :, 0], -1.0, rstd[:, at], ALU.mult, ALU.mult).then_inc(norm_done, 1)

            def take(c, b, first):
                dve.wait_ge(node_mm, c * CHUNK + b + 1)
                if not first and b == 0:
                    dve.wait_ge(table_out, c * 16)
                pair = ps_w[:, b % 2, 0:2, :]
                at = bass.ds(c * CHUNK + b, 1)
                nc.vector.tensor_scalar(l_st[:, b, :], pair[:, 0, 0:C], a_sb[:, at], None, ALU.mult).then_inc(l_done, 1)
                xr = xres[:, at, :].rearrange("p b c -> p (b c)")
                nc.vector.scalar_tensor_tensor(xr, pair[:, 1, 0:C], a_sb[:, at], xr, ALU.mult, ALU.add).then_inc(res_done, 1)

            dve.wait_ge(ld_x, 16)
            statistics(0, range(CHUNK))
            aggregate(0)
            dve.wait_ge(ld_wnode, 32)
            for part, scale in ((wnode[:, :, 0:MUL0], MUL0 ** -0.5), (wnode[:, :, MUL0:P], MUL1 ** -0.5),
                                (wnode_z[:, :, :], MUL1 ** -0.5)):
                nc.vector.tensor_scalar(part, part, float(scale), None, ALU.mult).then_inc(w_scaled, 1)
            normalizers(0)

            dve.wait_ge(ld_dst, 16)
            nc.vector.tensor_copy(dst_rel[:, :], dst_i[:, :]).then_inc(dst_step, 1)
            nc.vector.tensor_copy(base_i[:, :], dst_i[0:1, 0:TILES:T])
            nc.vector.tensor_copy(base_f[:, :], dst_i[0:1, 0:TILES:T]).then_inc(dst_step, 1)
            dve.wait_ge(ld_w, 48)
            for part, scale in ((w_out[0:3 * MUL1, 3, :], K_SUM), (w_out[:, 0:3, :], K_SUM),
                                (w_out[3 * MUL1:P, 3, :], K_SUM * K_DOT)):
                nc.vector.tensor_scalar(part, part, float(scale), None, ALU.mult).then_inc(w_scaled, 1)
            dve.wait_ge(base_bc, 1)
            dve.wait_ge(dst_step, 2)
            by_group = dst_rel[:, :].rearrange("p (g t) -> p g t", t=T)
            nc.vector.tensor_tensor(by_group, by_group, ps_s[:, 0, 0:GROUPS].unsqueeze(2).to_broadcast([P, GROUPS, T]),
                                    ALU.subtract).then_inc(dst_step, 1)
            dve.wait_ge(ld_a, 16)

            def path_flag():
                dve.wait_ge(dst_step, 3)
                nc.vector.tensor_reduce(span[:, 0:1], dst_rel[:, :], AX.X, ALU.max).then_inc(dst_step, 1)
                nc.vector.tensor_reduce(span[:, 1:2], dst_rel[:, :], AX.X, ALU.min).then_inc(dst_step, 1)
                dve.wait_ge(order_step, 3)
                nc.vector.tensor_reduce(span[:, 2:3], above, AX.X, ALU.min).then_inc(dst_step, 1)
                dve.wait_ge(dst_step, 6)
                nc.vector.tensor_scalar(span[:, 3:4], span[:, 0:1], float(W) - 0.5, None, ALU.is_gt).then_inc(dst_step, 1)
                nc.vector.tensor_scalar(span[:, 4:6], span[:, 1:3], -0.5, None, ALU.is_lt).then_inc(dst_step, 1)
                dve.wait_ge(flag_sum, 1)
                nc.vector.tensor_copy(flag_i[:, :], ps_s[0:1, 0, 0:1]).then_inc(flag_set, 1)

            def chunk(c, first, last):
                if not last:
                    dve.wait_ge(ld_x, c * 16 + 32)
                for b in range(CHUNK):
                    if not last and b < 4:
                        statistics(c + 1, range(2 * b, min(2 * b + 2, CHUNK)))
                    if not last and b == 4:
                        aggregate(c + 1)
                    if not last and b == 6:
                        normalizers(c + 1)
                    take(c, b, first)

            chunk(0, True, False)
            with dve.Fori(1, CHUNKS - 1) as c:
                chunk(c, False, False)
            chunk(CHUNKS - 1, False, True)
            path_flag()
            dve.wait_ge(consts, 9)
            dve.wait_ge(zeroed, 1)

            def attr_of(j, a, b):
                return attr_sb[:, j // HALF, (j % HALF) * T:(j % HALF) * T + T, a:b]

            def edge_dots(j):
                nc.vector.tensor_tensor(dots[:, :, :, :], vectors(j), attr_of(j, 1, 4).unsqueeze(3).to_broadcast([P, T, 3, MUL1]),
                                        ALU.mult).then_inc(dots_done, 1)

            def sum_dots():
                nc.vector.tensor_reduce(dot[:, :, :], dots[:, :, :, :].rearrange("p t d u -> p t u d"), AX.X, ALU.add).then_inc(dot_done, 1)

            def vectors(j):
                return y[:, j, :, MUL0:C].rearrange("p t (d u) -> p t d u", d=3)

            def scalar_products(j, s):
                nc.vector.tensor_tensor(msg[:, s, :, 0:2 * MUL0].rearrange("p t (k u) -> p t k u", k=2),
                                        ps_w[:, s, :, 0:2 * MUL0].rearrange("p t (k u) -> p t k u", k=2),
                                        y[:, j, :, 0:MUL0].unsqueeze(2).to_broadcast([P, T, 2, MUL0]), ALU.mult).then_inc(msg_done, 1)

            def vector_products(j, s):
                nc.vector.tensor_tensor(msg[:, s, :, 2 * MUL0:M - MUL1].rearrange("p t (d u) -> p t d u", d=3),
                                        ps_w[:, s, :, 2 * MUL0:NW - MUL1].unsqueeze(2).to_broadcast([P, T, 3, MUL1]),
                                        vectors(j), ALU.mult).then_inc(msg_done, 1)

            def dot_products(s):
                nc.vector.tensor_tensor(msg[:, s, :, M - MUL1:M], ps_w[:, s, :, NW - MUL1:NW], dot[:, :, :], ALU.mult).then_inc(msg_done, 1)

            def messages(i, j):
                g, s = i * G + j, j % 2
                if j % HALF == 0:
                    dve.wait_ge(ld_attr[j // HALF], i * 16 + 16)
                nc.vector.tensor_tensor(hot[:, s, :, 0, :], iota_w[:, :].unsqueeze(1).to_broadcast([P, T, W]),
                                        dst_rel[:, bass.ds(g * T, T)].unsqueeze(2).to_broadcast([P, T, W]),
                                        ALU.is_equal).then_inc(hot_done, 1)
                dve.wait_ge(gathered[j], i * (16 * T) + 16 * T)
                edge_dots(j)
                dve.wait_ge(hot_done, g + 1)
                nc.vector.tensor_tensor(hot[:, s, :, 1:V, :], hot[:, s, :, 0:1, :].to_broadcast([P, T, 4, W]),
                                        attr_of(j, 0, 4).unsqueeze(3).to_broadcast([P, T, 4, W]), ALU.mult).then_inc(msg_done, 1)
                dve.wait_ge(dots_done, g + 1)
                sum_dots()
                dve.wait_ge(fc2_done, g + 1)
                scalar_products(j, s)
                vector_products(j, s)
                dve.wait_ge(dot_done, g + 1)
                dot_products(s)

            def finish(b, frm):
                xr = xres[:, bass.ds(b, 1), :].rearrange("p b c -> p (b c)")
                nc.vector.scalar_tensor_tensor(xr, frm, a_sb[:, bass.ds(b, 1)], xr, ALU.mult, ALU.add).then_inc(fin_done, 1)

            def accumulate(g, s, base, first, block=None):
                dve.wait_ge(win_done, g + 1)
                if block is not None:
                    finish(block, ps_s[:, s, FIN:FIN + C])
                if not first:
                    dve.wait_ge(acc_done, g * 4)
                p = ps_s[:, s, :]
                for rows, slots, cols in ((slice(0, MUL0), slice(0, 1), slice(0, W)),
                                          (slice(MUL0, P), slice(0, 3), slice(W, 4 * W)),
                                          (slice(0, 3 * MUL1), slice(3, 4), slice(5 * W, 6 * W)),
                                          (slice(3 * MUL1, P), slice(3, 4), slice(4 * W, 5 * W))):
                    to = acc[rows, slots, bass.ds(base, W)]
                    nc.vector.tensor_tensor(to, to, p[rows, cols].rearrange("p (v n) -> p v n", n=W), ALU.add).then_inc(acc_done, 1)

            def base_of(g):
                return dve.value_load(base_i[0:1, bass.ds(g, 1)], min_val=0, max_val=N - 1)

            def windowed():
                def pair(k, first, last_of_block):
                    for j in range(2 * G):
                        g = k * (2 * G) + j
                        messages(k * 2 + j // G, j % G)
                        if j >= 1 or not first:
                            accumulate(g - 1, (j - 1) % 2, base_of(g - 1), first and j == 1,
                                       k - LAG if last_of_block and j == 6 else None)

                pair(0, True, False)
                with dve.Fori(1, LAG) as k:
                    pair(k, False, False)
                with dve.Fori(LAG, PAIRS) as k:
                    pair(k, False, True)
                for j in range(G):
                    g = (TURNS - 1) * G + j
                    messages(TURNS - 1, j)
                    accumulate(g - 1, (j - 1) % 2, base_of(g - 1), False)
                accumulate(GROUPS - 1, (GROUPS - 1) % 2, base_of(GROUPS - 1), False)
                for b in range(IN_LOOP, BLOCKS):
                    dve.wait_ge(fin_mm, b + 1)
                    finish(b, ps_w[:, b % 2, 0, 0:C])

            def general():
                nc.vector.memset(full, 0.0)
                dve.sem_inc(g_free, 1)
                with dve.Fori(0, GROUPS) as g:
                    dve.wait_ge(g_loaded, g * 48 + 48)
                    dve.wait_ge(g_rows, g * (16 * T) + 16 * T)
                    edge_dots(0)
                    dve.drain()
                    sum_dots()
                    dve.wait_ge(g_fc2, g + 1)
                    scalar_products(0, 0)
                    vector_products(0, 0)
                    dve.drain()
                    dot_products(0)
                    for t in range(T):
                        n = g * T + t
                        nc.vector.tensor_copy(dst_col[:, :], dst_i[:, bass.ds(n, 1)])
                        dve.drain()
                        nc.vector.tensor_copy(dst_bc, dst_col[:, :].to_broadcast([P, P])).then_inc(g_col, 1)
                        dve.drain()
                        part = msg[:, 0, t, :]
                        for at, frm, k in ((0, slice(0, MUL0), 0), (MUL0, slice(MUL0, 2 * MUL0), 1),
                                           (P + MUL0, slice(MUL0, 2 * MUL0), 2), (2 * P + MUL0, slice(MUL0, 2 * MUL0), 3),
                                           (3 * P, slice(2 * MUL0, M - MUL1), 0)):
                            nc.vector.tensor_scalar(full[:, at:at + frm.stop - frm.start], part[:, frm],
                                                    attr_sb[:, 0, t, k:k + 1], None, ALU.mult)
                        nc.vector.tensor_copy(full[:, 4 * P - MUL1:4 * P], part[:, M - MUL1:M])
                        dve.wait_ge(g_turned, n + 1)
                        nc.vector.tensor_tensor(same, ps_s[:, 0, 0:P], dst_col[:, :].to_broadcast([P, P]), ALU.is_equal)
                        dve.drain()
                        dve.sem_inc(g_full, 1)
                        nc.vector.tensor_tensor(same_before, same, lower[:, :], ALU.mult)
                        nc.vector.tensor_tensor(away[:, :], trash[:, :], dst_col[:, :], ALU.subtract)
                        dve.drain()
                        nc.vector.tensor_reduce(repeats[:, :], same_before, AX.X, ALU.max)
                        dve.drain()
                        nc.vector.tensor_tensor(away[:, :], away[:, :], repeats[:, :], ALU.mult)
                        dve.drain()
                        dve.wait_ge(g_turn, n + 1)
                        nc.vector.tensor_tensor(idx_sum[:, :], away[:, :], dst_col[:, :], ALU.add)
                        dve.wait_ge(g_summed, n + 1)
                        nc.vector.tensor_copy(sums, ps_s[:, 1, :])
                        dve.drain()
                        dve.sem_inc(g_taken, 1)
                    dve.sem_inc(g_free, 1)
                dve.sem_inc(g_block_free, 1)
                with dve.Fori(0, BLOCKS) as b:
                    dve.wait_ge(g_block_turned, b + 1)
                    nc.vector.tensor_copy(acc[:, :, bass.ds(b * P, P)], ps_w[:, 0, :, 0:P]).then_inc(g_block_free, 1)
                with dve.Fori(0, BLOCKS) as b:
                    dve.wait_ge(fin_mm, b + 1)
                    finish(b, ps_w[:, 0, 0, 0:C])

            by_path(dve, windowed, general)

        @block.tensor
        def _(pe):
            pe.wait_ge(consts, 9)
            pe.wait_ge(dst_step, 2)
            nc.tensor.matmul(ps_s[:, 0, 0:GROUPS], ones[0:1, :], base_f[:, :], start=True, stop=True).then_inc(base_bc, 1)
            pe.wait_ge(w_scaled, 3)
            pe.wait_ge(dst_step, 3)

            def had_bank(b):
                return b - 2 if b >= 2 else -1 - b

            def chunk(c, first):
                def turn_block(b):
                    pe.wait_ge(hid_done, c * CHUNK + b + 1)
                    if b >= 2 or not first:
                        pe.wait_ge(hidt_done, c * CHUNK + had_bank(b) + 1)
                    nc.tensor.transpose(ps_h[:, b % 2, 0:P], hid[:, b, 0:P], ident[:, :])
                    nc.tensor.transpose(ps_s[0:MUL1, b % 2, 0:P], hid[:, b, P:C], ident[:, :]).then_inc(tr_done, 1)

                def linear(b):
                    pe.wait_ge(hidt_done, c * CHUNK + b + 1)
                    if b >= 2 or not first:
                        before = c * CHUNK + had_bank(b)
                        pe.wait_ge(l_done, before + 1)
                        pe.wait_ge(res_done, before + 1)
                    pair = ps_w[:, b % 2, 0:2, :]
                    nc.tensor.matmul(pair[:, :, 0:P], hid_t[:, b, 0, :], wnode[:, :, :], start=True, stop=True)
                    nc.tensor.matmul(pair[:, :, P:C], hid_t[0:MUL1, b, 1, :], wnode_z[:, :, :], start=True, stop=True).then_inc(node_mm, 1)

                for b in range(CHUNK):
                    turn_block(b)
                    if b >= 1:
                        linear(b - 1)
                linear(CHUNK - 1)

            chunk(0, True)
            with pe.Fori(1, CHUNKS) as c:
                chunk(c, False)

            pe.wait_ge(dst_step, 8)
            for n in range(3):
                ins = nc.tensor.matmul(ps_s[0:1, 0, 0:1], ones[:, 0:1], span[:, 3 + n:4 + n], start=(n == 0), stop=(n == 2))
            ins.then_inc(flag_sum, 1)
            pe.wait_ge(w_scaled, 6)

            def fc1(i, j):
                if j % HALF == 0:
                    pe.wait_ge(ld_rad[j // HALF], i * 16 + 16)
                nc.tensor.matmul(ps_h[0:N_RADIAL, j % 2, 0:GE], w_fc1[:, :], rad[:, j // HALF, (j % HALF) * GE:(j % HALF + 1) * GE],
                                 start=True, stop=True).then_inc(fc1_done, 1)

            def fc2(g, s):
                pe.wait_ge(relu_done, g + 1)
                for t in range(T):
                    ins = nc.tensor.matmul(ps_w[:, s, t, 0:NW], hr[:, s, t * P:(t + 1) * P], w_fc2[:, :], start=True, stop=True)
                ins.then_inc(fc2_done, 1)

            def last_linear(b, o):
                pe.wait_ge(fin_copied, b + 1)
                nc.tensor.matmul(o[:, 0:C], fin_in[:, 3, :], w_out[:, 3, :], start=True, stop=False)
                nc.tensor.matmul(o[:, 0:MUL0 + MUL1], fin_in[:, 0, :], w_out[:, 0, 0:MUL0 + MUL1], start=False, stop=False)
                for d in (1, 2):
                    at = slice(MUL0 + MUL1 * d, MUL0 + MUL1 * (d + 1))
                    ins = nc.tensor.matmul(o[:, at], fin_in[:, d, :], w_out[:, d, at], start=False, stop=(d == 2))
                ins.then_inc(fin_mm, 1)

            def windows(g, s, first, block=None):
                pe.wait_ge(msg_done, g * 4 + 4)
                if not first:
                    pe.wait_ge(acc_done, (g - 1) * 4)
                if block is not None:
                    last_linear(block, ps_s[:, s, FIN:FIN + C])
                for t in range(T):
                    nc.tensor.matmul(ps_s[:, s, 0:4 * W], msg[:, s, t, 0:P], hot[:, s, t, 1:V, :], start=(t == 0), stop=(t == T - 1))
                for t in range(T):
                    ins = nc.tensor.matmul(ps_s[:, s, 4 * W:6 * W], msg[:, s, t, P:M], hot[:, s, t, 0:2, :], start=(t == 0), stop=(t == T - 1))
                ins.then_inc(win_done, 1)

            def node_stage_left():
                pe.wait_ge(l_done, BLOCKS)
                pe.wait_ge(res_done, BLOCKS)

            def windowed():
                def pair(k, first, finish):
                    for j in range(2 * G):
                        g = k * (2 * G) + j
                        fc1(k * 2 + j // G, j % G)
                        if first and j == 1:
                            node_stage_left()
                        if j >= 1 or not first:
                            fc2(g - 1, (j - 1) % 2)
                        if j >= 2 or not first:
                            windows(g - 2, j % 2, first and j < 4, k - LAG if finish and j == 7 else None)

                pair(0, True, False)
                with pe.Fori(1, LAG) as k:
                    pair(k, False, False)
                with pe.Fori(LAG, PAIRS) as k:
                    pair(k, False, True)
                for j in range(G):
                    g = (TURNS - 1) * G + j
                    fc1(TURNS - 1, j)
                    fc2(g - 1, (j - 1) % 2)
                    windows(g - 2, j % 2, False)
                fc2(GROUPS - 1, (GROUPS - 1) % 2)
                windows(GROUPS - 2, 0, False)
                windows(GROUPS - 1, 1, False)
                for b in range(IN_LOOP, BLOCKS):
                    last_linear(b, ps_w[:, b % 2, 0, :])

            def general():
                node_stage_left()
                with pe.Fori(0, GROUPS) as g:
                    pe.wait_ge(g_loaded, g * 48 + 48)
                    nc.tensor.matmul(ps_h[0:N_RADIAL, 0, 0:GE], w_fc1[:, :], rad[:, 0, 0:GE], start=True, stop=True).then_inc(g_fc1, 1)
                    pe.wait_ge(g_relu, g + 1)
                    for t in range(T):
                        ins = nc.tensor.matmul(ps_w[:, 0, t, 0:NW], hr[:, 0, t * P:(t + 1) * P], w_fc2[:, :], start=True, stop=True)
                    ins.then_inc(g_fc2, 1)
                    for t in range(T):
                        n = g * T + t
                        pe.wait_ge(g_col, n + 1)
                        nc.tensor.transpose(ps_s[:, 0, 0:P], dst_bc, ident[:, :]).then_inc(g_turned, 1)
                        pe.wait_ge(g_full, n + 1)
                        nc.tensor.matmul(ps_s[:, 1, :], same, full, start=True, stop=True).then_inc(g_summed, 1)
                with pe.Fori(0, BLOCKS) as b:
                    pe.wait_ge(g_block_in, b * 16 + 16)
                    for v in range(4):
                        ins = nc.tensor.transpose(ps_w[:, 0, v, 0:P], rows_in[:, v * P:(v + 1) * P], ident[:, :])
                    ins.then_inc(g_block_turned, 1)

                last_linear(0, ps_w[:, 0, 0, :])
                with pe.Fori(1, BLOCKS) as b:
                    pe.wait_ge(fin_done, b)
                    last_linear(b, ps_w[:, 0, 0, :])

            by_path(pe, windowed, general)


ORDER = np.concatenate([np.arange(MUL0)] + [MUL0 + 3 * np.arange(MUL1) + d for d in range(3)])


def kernel(**inputs):
    import concourse.bacc as bacc
    from concourse.bass_utils import run_bass_kernel_spmd

    get = {k: np.asarray(v) for k, v in inputs.items()}

    def by_tile(v, fill):
        padded = np.concatenate([v, np.broadcast_to(fill, (EP - E, *v.shape[1:])).astype(v.dtype)])
        return np.ascontiguousarray(np.moveaxis(padded.reshape(TILES, P, *v.shape[1:]), 0, 1))

    def padded_rows(v):
        return np.concatenate([v, np.zeros((NP - N, v.shape[1]), v.dtype)])

    radial = np.zeros((N_BASIS, EP), np.float32)
    radial[:, :E] = get["edge_attr_10"].T
    arrays = {
        "x": np.ascontiguousarray(padded_rows(get["x"])[:, ORDER]),
        "src": by_tile(get["src"], 0),
        "dst": by_tile(get["dst"], get["dst"][-1]),
        "radial": radial,
        "attr": by_tile(get["edge_attr_4"], 0),
        "avec": np.ascontiguousarray(padded_rows(get["node_vec1"]).reshape(BLOCKS, P).T),
    }
    w = {k[7:]: v for k, v in get.items() if k.startswith("L0_gnn_")}
    w_node = np.zeros((P, 2, P), np.float32)
    w_last = np.zeros((P, 4, C), np.float32)
    w_last[:MUL0, 0, :MUL0] = w["W_l2_00"]
    w_last[3 * MUL1:, 3, :MUL0] = w["W_l2_10"]
    for n, (w0, w1) in enumerate((("W_l1_0", "W_l1_1"), ("W_si0", "W_si1"))):
        w_node[:MUL0, n, :MUL0] = w[w0]
        for d in range(2):
            at = slice(MUL0 + MUL1 * d, MUL0 + MUL1 * (d + 1))
            w_node[at, n, at] = w[w1]
    for d in range(3):
        at = slice(MUL0 + MUL1 * d, MUL0 + MUL1 * (d + 1))
        w_last[MUL0:, d, at] = w["W_l2_01"]
        w_last[MUL1 * d:MUL1 * (d + 1), 3, at] = w["W_l2_11"]
    arrays["w_node"] = w_node
    arrays["w_node_z"] = np.ascontiguousarray(np.stack([w["W_l1_1"], w["W_si1"]], axis=1))
    arrays["w_last"] = w_last
    arrays["w_fc1"] = np.ascontiguousarray(w["W_fc1"])
    arrays["w_fc2"] = np.ascontiguousarray(w["W_fc2"])
    nc = bacc.Bacc("TRN2", target_bir_lowering=False, num_devices=1)
    args = [nc.dram_tensor(f"in_{k}", a.shape, mybir.dt.from_np(a.dtype), kind="ExternalInput").ap() for k, a in arrays.items()]
    args.append(nc.dram_tensor("out", (NP, C), F32, kind="ExternalOutput").ap())
    gnn_layer(nc, *args)
    r = run_bass_kernel_spmd(nc, [{f"in_{k}": a for k, a in arrays.items()}], core_ids=[0])
    rows = np.asarray(r.results[0]["out"])[:N]
    result = np.empty_like(rows)
    result[:, ORDER] = rows
    return result
```

```python
import numpy as np
import concourse.bass as bass
from concourse import mybir
from contextlib import ExitStack

P = 128
N = 6250
E = 206250
MUL0, MUL1 = 64, 32
C = MUL0 + 3 * MUL1
N_BASIS, N_RADIAL = 10, 100
NW = 2 * MUL0 + 2 * MUL1
BLOCKS = -(-N // P)
CHUNK = 7
CHUNKS = BLOCKS // CHUNK
assert CHUNKS % 2
STORES = CHUNKS + 1
Z = MUL0 + 2 * MUL1
assert Z == P
Z_BLOCKS = [(0, P // MUL1), (P // MUL1, CHUNK)]
assert CHUNKS * CHUNK == BLOCKS
NP = BLOCKS * P

T = 4
W = 32
V = 5
G = 4
HALF = 2
TURNS = -(-E // (P * T * G))
GROUPS = TURNS * G
TILES = GROUPS * T
EDGE_GROUPS = -(-E // (P * T))
LEFT = EDGE_GROUPS - (TURNS - 1) * G
PAIRS = TURNS // 2
assert TURNS == 2 * PAIRS + 1
LAG = 3
IN_LOOP = PAIRS - LAG
assert IN_LOOP == BLOCKS - 2 and 2 <= LEFT
FIN = 6 * W
EP = TILES * P
GE = T * P
NA = N + W
M = 2 * P
TRASH = NP
ND = NP + P

EPS = 1e-5
K_RADIAL = float(np.sqrt(2.0) / np.sqrt(N_BASIS))
K_SUM = float(0.5 / np.sqrt(16.0) / np.sqrt(MUL0 + MUL1) / np.sqrt(N_RADIAL))
K_DOT = float(1.0 / np.sqrt(3.0))

F32 = mybir.dt.float32
I32 = mybir.dt.int32
ALU = mybir.AluOpType
ACT = mybir.ActivationFunctionType
AX = mybir.AxisListType


def gnn_layer(nc, x, src, dst, radial, attr, avec, w_lin, w_lin_z, w_self, w_self_z, w_last, wf1, wf2, out):
    ctx = ExitStack()
    with ctx:
        def sb(name, shape, dt=F32):
            return ctx.enter_context(nc.sbuf_tensor(name, shape, dt))

        def sem(name):
            return ctx.enter_context(nc.semaphore(name))

        table = nc.dram_tensor("table", (NP, C), F32).ap()
        sums_d = nc.dram_tensor("sums_d", (ND, 4 * P), F32).ap()

        acc = sb("acc", [P, 4, NA])
        xres = sb("xres", [P, BLOCKS, C])
        a_sb = sb("a_sb", [P, BLOCKS])
        dst_i = sb("dst_i", [P, TILES], I32)
        dst_rel = sb("dst_rel", [P, TILES])
        base_f = sb("base_f", [1, GROUPS])
        base_i = sb("base_i", [1, GROUPS], I32)
        iota_i = sb("iota_i", [P, W], I32)
        iota_w = sb("iota_w", [P, W])
        ident = sb("ident", [P, P])
        ones = sb("ones", [P, P])
        span = sb("span", [P, 6])
        flag_i = sb("flag_i", [1, 1], I32)
        wl = sb("wl", [P, P])
        wlz = sb("wlz", [P, P])
        wself = sb("wself", [P, P])
        wselfz = sb("wselfz", [MUL1, MUL1])
        w_fc1 = sb("w_fc1", [N_BASIS, N_RADIAL])
        w_fc2 = sb("w_fc2", [N_RADIAL, NW])
        w_out = sb("w_out", [P, 4, C])
        stats = sb("stats", [P, CHUNK, 6])
        mean_var = sb("mean_var", [P, CHUNK, 2])
        eps = sb("eps", [P, 1])
        std = sb("std", [P, CHUNK])
        early = sb("early", [P, 1])
        rstd = sb("rstd", [P, BLOCKS])
        shift = sb("shift", [P, BLOCKS])
        hid = sb("hid", [P, CHUNK, Z])
        hid_zs = sb("hid_zs", [P, CHUNK * MUL1])
        hid_t = sb("hid_t", [P, CHUNK, P])
        hid_z = sb("hid_z", [P, 2, P])
        idx = sb("idx", [P, 2, HALF * T], I32)
        attr_sb = sb("attr_sb", [P, 2, HALF * T, 4])
        rad = sb("rad", [N_BASIS, 2, HALF * GE])
        y = sb("y", [P, G, T, C])
        hr = sb("hr", [N_RADIAL, 2, GE])
        msg = sb("msg", [P, 2, T, M])
        hot = sb("hot", [P, 2, T, V, W])
        dots = sb("dots", [P, T, 3, MUL1])
        dot = sb("dot", [P, T, MUL1])
        fin_in = sb("fin_in", [P, 4, P])
        l_st = y[:, :, :, :].rearrange("p g t c -> p (g t c)")[:, 0:2 * CHUNK * C].rearrange("p (n b c) -> p n b c", n=2, b=CHUNK)
        least = acc[:, 0, 0:TILES].bitcast(I32)
        above = msg[:, :, :, :].rearrange("p s t m -> p (s t m)")[:, 0:TILES].bitcast(I32)
        spare = msg[:, 1, :, :].rearrange("p t m -> p (t m)")
        full, sums = spare[:, 0:4 * P], spare[:, 4 * P:8 * P]
        spare = hot[:, 1, :, :, :].rearrange("p t v w -> p (t v w)")
        same, same_before, dst_bc = (spare[:, n * P:(n + 1) * P] for n in range(3))
        lower = sb("lower", [P, P])
        dst_col = sb("dst_col", [P, 1])
        repeats = sb("repeats", [P, 1])
        trash_i = sb("trash_i", [P, 1], I32)
        trash = sb("trash", [P, 1])
        away = sb("away", [P, 1])
        idx_sum = sb("idx_sum", [P, 1], I32)
        rows_in = y[:, 0, :, :].rearrange("p t c -> p (t c)")[:, 0:4 * P]

        def ps(name, shape):
            return ctx.enter_context(nc.psum_tensor(name, shape, F32))

        ps_h = ps("ps_h", [P, 2, 512])
        ps_w = ps("ps_w", [P, 2, T, 256])
        ps_s = ps("ps_s", [P, 2, 512])

        sp_passed, dve_passed, pool_passed = sem("sp_passed"), sem("dve_passed"), sem("pool_passed")
        ld_x = sem("ld_x")
        ld_dst = sem("ld_dst")
        ld_a = sem("ld_a")
        ld_w = sem("ld_w")
        ld_wnode = sem("ld_wnode")
        zeroed = sem("zeroed")
        consts = sem("consts")
        dst_step = sem("dst_step")
        base_bc = sem("base_bc")
        flag_sum = sem("flag_sum")
        flag_set = sem("flag_set")
        order_step = sem("order_step")
        w_scaled = sem("w_scaled")
        bn_done = sem("bn_done")
        aggr_done = sem("aggr_done")
        std_done = sem("std_done")
        rstd_done = sem("rstd_done")
        norm_done = sem("norm_done")
        hid_done = sem("hid_done")
        tr_done = sem("tr_done")
        trz_done = sem("trz_done")
        hidt_done = sem("hidt_done")
        hidz_done = sem("hidz_done")
        node_mm = sem("node_mm")
        node_mm_z = sem("node_mm_z")
        l_done = sem("l_done")
        lz_done = sem("lz_done")
        table_out = sem("table_out")
        ld_idx = [sem(f"ld_idx{c}") for c in range(2)]
        ld_attr = [sem(f"ld_attr{c}") for c in range(2)]
        ld_rad = [sem(f"ld_rad{c}") for c in range(2)]
        gathered = [sem(f"gathered{j}") for j in range(G)]
        fc1_done = sem("fc1_done")
        relu_done = sem("relu_done")
        fc2_done = sem("fc2_done")
        hot_done = sem("hot_done")
        dots_done = sem("dots_done")
        dot_done = sem("dot_done")
        msg_done = sem("msg_done")
        win_done = sem("win_done")
        acc_done = sem("acc_done")
        g_zeroed, g_free, g_loaded, g_rows, g_fc1, g_relu, g_fc2 = (
            sem("g_" + n) for n in ("zeroed", "free", "loaded", "rows", "fc1", "relu", "fc2"))
        g_col, g_turned, g_full, g_summed, g_taken, g_added, g_turn = (
            sem("g_" + n) for n in ("col", "turned", "full", "summed", "taken", "added", "turn"))
        g_block_free, g_block_in, g_block_turned = (sem("g_block_" + n) for n in ("free", "in", "turned"))
        fin_copied = sem("fin_copied")
        fin_mm = sem("fin_mm")
        fin_done = sem("fin_done")
        stored = sem("stored")

        table_v = table.rearrange("(b p) c -> p b c", p=P)
        x_v = x.rearrange("(b p) c -> p b c", p=P)
        out_v = out.rearrange("(b p) c -> p b c", p=P)

        base_ps = ps_w[:, 0, 2:4, :].rearrange("p a c -> p (a c)")
        flag_ps = ps_w[0:1, 1, 3, 0:1]

        def last_products(b):
            return ps_w[:, (EDGE_GROUPS - 2 + b - IN_LOOP) % 2, 0, 0:C]

        def by_path(eng, windowed, general):
            eng.wait_ge(flag_set, 1)
            outside = eng.value_load(flag_i[0:1, 0:1], min_val=0, max_val=3 * P)
            with eng.If(outside):
                general()
            with eng.Else():
                windowed()

        block = ctx.enter_context(nc.Block())

        @block.sync
        def _(sp):
            def load_x(c, first):
                if not first:
                    sp.wait_ge(ld_x, 16 * c)
                    sp.sem_inc(sp_passed, 1)
                at = bass.ds(c * CHUNK, CHUNK)
                sp.dma_start(xres[:, at, :], x_v[:, at, :]).then_inc(ld_x, 16)

            load_x(0, True)
            with sp.Fori(1, CHUNKS) as c:
                load_x(c, False)

            def store_table(c, stores, parity, lo, hi):
                sp.wait_ge(l_done, c * CHUNK + hi)
                sp.wait_ge(lz_done, c * 2 + (1 if hi == Z_BLOCKS[0][1] else 2))
                sp.sem_inc(sp_passed, 1)
                if stores is not None:
                    sp.wait_ge(table_out, stores * 16)
                sp.dma_start(table_v[:, bass.ds(c * CHUNK + lo, hi - lo), :], l_st[:, parity, lo:hi, :]).then_inc(table_out, 16)

            store_table(0, None, 0, 0, CHUNK)
            store_table(1, 1, 1, 0, CHUNK)
            with sp.Fori(1, CHUNKS // 2) as t:
                for parity in range(2):
                    store_table(t * 2 + parity, t * 2 + parity, parity, 0, CHUNK)
            for n, (lo, hi) in enumerate(Z_BLOCKS):
                store_table(CHUNKS - 1, CHUNKS - 1 + n, (CHUNKS - 1) % 2, lo, hi)

            def store_out(c, lo, hi):
                sp.wait_ge(fin_done, c * CHUNK + hi)
                sp.sem_inc(sp_passed, 1)
                at = bass.ds(c * CHUNK + lo, hi - lo)
                sp.dma_start(out_v[:, at, :], xres[:, at, :]).then_inc(stored, 16)

            def store_rest(begin):
                with sp.Fori(begin, CHUNKS - 1) as c:
                    store_out(c, 0, CHUNK)
                store_out(CHUNKS - 1, 0, CHUNK - 1)
                store_out(CHUNKS - 1, CHUNK - 1, CHUNK)

            def load_half(i, c, first):
                k = i * 2 + c
                if not first:
                    sp.wait_ge(fc1_done, (k - 1) * HALF)
                    sp.sem_inc(sp_passed, 1)
                sp.dma_start(rad[:, c, :], radial[:, bass.ds(k * HALF * GE, HALF * GE)]).then_inc(ld_rad[c], 16)
                if not first:
                    for j in range(HALF * c, HALF * c + HALF):
                        sp.wait_ge(gathered[j], i * (16 * T))
                    sp.sem_inc(sp_passed, 1)
                sp.dma_start(idx[:, c, :], src[:, bass.ds(k * HALF * T, HALF * T)]).then_inc(ld_idx[c], 16)
                if not first:
                    sp.wait_ge(msg_done, (k - 1) * HALF * 4)
                    sp.sem_inc(sp_passed, 1)
                sp.dma_start(attr_sb[:, c, :, :], attr[:, bass.ds(k * HALF * T, HALF * T), :]).then_inc(ld_attr[c], 16)

            def windowed():
                for c in range(2):
                    load_half(0, c, True)
                half_way = TURNS // 2
                with sp.Fori(1, half_way) as i:
                    for c in range(2):
                        load_half(i, c, False)
                early = (half_way // 2 - LAG - 1) // CHUNK
                for c in range(early):
                    store_out(c, 0, CHUNK)
                with sp.Fori(half_way, TURNS) as i:
                    for c in range(2):
                        load_half(i, c, False)
                store_rest(early)

            def general():
                sp.wait_ge(zeroed, 1)
                with sp.Fori(0, ND // P) as b:
                    sp.dma_start(sums_d[bass.ds(b * P, P), :], acc[:, 0, 0:4 * P]).then_inc(g_zeroed, 16)
                with sp.Fori(0, GROUPS) as g:
                    sp.wait_ge(g_free, g + 1)
                    sp.sem_inc(sp_passed, 1)
                    sp.dma_start(rad[:, 0, 0:GE], radial[:, bass.ds(g * GE, GE)]).then_inc(g_loaded, 16)
                    sp.dma_start(idx[:, 0, 0:T], src[:, bass.ds(g * T, T)]).then_inc(g_loaded, 16)
                    sp.dma_start(attr_sb[:, 0, 0:T, :], attr[:, bass.ds(g * T, T), :]).then_inc(g_loaded, 16)
                sp.wait_ge(g_turn, TILES + 1)
                with sp.Fori(0, BLOCKS) as b:
                    sp.wait_ge(g_block_free, b + 1)
                    sp.sem_inc(sp_passed, 1)
                    sp.dma_start(rows_in, sums_d[bass.ds(b * P, P), :]).then_inc(g_block_in, 16)
                store_rest(0)

            by_path(sp, windowed, general)

            sp.wait_ge(stored, 16 * STORES)

        @block.gpsimd
        def _(pool):
            nc.gpsimd.memset(ident[:, :], 0.0).then_inc(consts, 1)
            nc.gpsimd.memset(ones[:, :], 1.0).then_inc(consts, 1)
            nc.gpsimd.memset(eps[:, :], EPS).then_inc(consts, 1)
            nc.gpsimd.iota(iota_i[:, :], pattern=[[1, W]], base=0, channel_multiplier=0).then_inc(consts, 1)
            pool.wait_ge(consts, 4)
            nc.gpsimd.affine_select(out=ident[:, :], in_=ident[:, :], compare_op=ALU.not_equal, fill=1.0, base=0,
                                    pattern=[[-1, P]], channel_multiplier=1).then_inc(consts, 1)
            nc.gpsimd.tensor_copy(iota_w[:, :], iota_i[:, :]).then_inc(consts, 1)
            nc.gpsimd.affine_select(out=lower[:, :], in_=ones[:, :], compare_op=ALU.is_gt, fill=0.0, base=0,
                                    pattern=[[-1, P]], channel_multiplier=1).then_inc(consts, 1)
            nc.gpsimd.iota(trash_i[:, :], pattern=[[1, 1]], base=TRASH, channel_multiplier=1).then_inc(consts, 1)
            pool.wait_ge(consts, 8)
            nc.gpsimd.tensor_copy(trash[:, :], trash_i[:, :]).then_inc(consts, 1)
            ramp = PAIRS * 2 * G * T
            nc.gpsimd.iota(least[:, 0:ramp], pattern=[[P, PAIRS], [0, ramp // PAIRS]], base=-P * (LAG - 1),
                           channel_multiplier=0).then_inc(order_step, 1)
            nc.gpsimd.iota(least[:, ramp:TILES], pattern=[[0, TILES - ramp]], base=P * (IN_LOOP + 1),
                           channel_multiplier=0).then_inc(order_step, 1)
            pool.wait_ge(order_step, 2)
            pool.wait_ge(ld_dst, 16)
            nc.gpsimd.tensor_tensor(above, dst_i[:, :], least, ALU.subtract).then_inc(order_step, 1)
            pool.wait_ge(order_step, 3)
            nc.gpsimd.memset(acc[:, :, :], 0.0).then_inc(zeroed, 1)
            pool.wait_ge(table_out, 16 * STORES)

            def gather_group(i, j, first):
                if j % HALF == 0:
                    pool.wait_ge(ld_idx[j // HALF], i * 16 + 16)
                if not first:
                    pool.wait_ge(msg_done, (i * G + j - G + 1) * 4)
                    pool.sem_inc(pool_passed, 1)
                for t in range(T):
                    col = (j % HALF) * T + t
                    nc.gpsimd.indirect_dma_start(
                        out=y[:, j, t, :], out_offset=None, in_=table,
                        in_offset=bass.IndirectOffsetOnAxis(ap=idx[:, j // HALF, col:col + 1], axis=0),
                    ).then_inc(gathered[j], 16)

            def windowed():
                for j in range(G):
                    gather_group(0, j, True)
                with pool.Fori(1, TURNS - 1) as i:
                    for j in range(G):
                        gather_group(i, j, False)
                for j in range(LEFT):
                    gather_group(TURNS - 1, j, False)

            def general():
                pool.wait_ge(g_zeroed, 16 * (ND // P))
                pool.sem_inc(g_turn, 1)
                with pool.Fori(0, GROUPS) as g:
                    pool.wait_ge(g_loaded, g * 48 + 48)
                    pool.sem_inc(pool_passed, 1)
                    for t in range(T):
                        nc.gpsimd.indirect_dma_start(
                            out=y[:, 0, t, :], out_offset=None, in_=table,
                            in_offset=bass.IndirectOffsetOnAxis(ap=idx[:, 0, t:t + 1], axis=0),
                        ).then_inc(g_rows, 16)
                    for t in range(T):
                        n = g * T + t
                        pool.wait_ge(g_taken, n + 1)
                        pool.sem_inc(pool_passed, 1)
                        nc.gpsimd.indirect_dma_start(
                            out=sums_d, out_offset=bass.IndirectOffsetOnAxis(ap=idx_sum[:, :], axis=0),
                            in_=sums, in_offset=None, compute_op=ALU.add,
                        ).then_inc(g_added, 16)
                        pool.wait_ge(g_added, n * 16 + 16)
                        pool.sem_inc(g_turn, 1)

            by_path(pool, windowed, general)

        @block.scalar
        def _(act):
            act.dma_start(wl[:, :], w_lin).then_inc(ld_wnode, 16)
            act.dma_start(wlz[:, :], w_lin_z).then_inc(ld_wnode, 16)
            act.dma_start(a_sb[:, :], avec).then_inc(ld_a, 16)
            act.dma_start(dst_i[:, :], dst).then_inc(ld_dst, 16)
            act.dma_start(wself[:, :], w_self).then_inc(ld_w, 16)
            act.dma_start(wselfz[:, :], w_self_z).then_inc(ld_w, 16)
            act.dma_start(w_out[:, :, :], w_last).then_inc(ld_w, 16)
            act.dma_start(w_fc1[:, :], wf1).then_inc(ld_w, 16)
            act.dma_start(w_fc2[:, :], wf2).then_inc(ld_w, 16)
            act.wait_ge(consts, 3)

            def deviation(c):
                act.wait_ge(aggr_done, c + 1)
                nc.scalar.activation(std[:, :], mean_var[:, :, 1], ACT.Sqrt, bias=eps[:, :], scale=1.0).then_inc(std_done, 1)

            def normalize(b, n):
                at = bass.ds(b, 1)
                for part, channels in ((hid[:, n, :], slice(0, Z)), (hid_zs[:, n * MUL1:(n + 1) * MUL1], slice(Z, C))):
                    ins = nc.scalar.activation(part, xres[:, at, channels].rearrange("p b c -> p (b c)"), ACT.Relu,
                                               bias=shift[:, at], scale=rstd[:, at])
                ins.then_inc(hid_done, 1)

            def chunk(c, last):
                def move(b):
                    act.wait_ge(tr_done, c * CHUNK + b + 1)
                    nc.scalar.activation(hid_t[:, b, :], ps_h[:, b % 2, 0:P], ACT.Copy).then_inc(hidt_done, 1)

                def move_z(q):
                    act.wait_ge(trz_done, c * 2 + q + 1)
                    rows = MUL1 * (Z_BLOCKS[q][1] - Z_BLOCKS[q][0])
                    nc.scalar.activation(hid_z[0:rows, q, :], ps_s[0:rows, q, 0:P], ACT.Copy).then_inc(hidz_done, 1)

                for b in range(CHUNK):
                    if b < CHUNK - 1:
                        normalize(c * CHUNK + b + 1, b + 1)
                    elif not last:
                        act.wait_ge(norm_done, c + 2)
                        normalize(c * CHUNK + CHUNK, 0)
                    if b == CHUNK - 1:
                        move_z(1)
                    move(b)
                    if b == 3:
                        move_z(0)
                        if not last:
                            deviation(c + 1)

            nc.scalar.activation(early[:, :], eps[:, :], ACT.Sqrt)
            deviation(0)
            act.wait_ge(norm_done, 1)
            normalize(0, 0)
            chunk(0, False)
            with act.Fori(1, CHUNKS - 1) as c:
                chunk(c, False)
            chunk(CHUNKS - 1, True)

            def relu(g, s, first):
                act.wait_ge(fc1_done, g + 1)
                if not first:
                    act.wait_ge(fc2_done, g - 1)
                nc.scalar.activation(hr[:, s, :], ps_h[0:N_RADIAL, s, 0:GE], ACT.Relu, scale=K_RADIAL).then_inc(relu_done, 1)

            def move_block(b, n, bank):
                act.wait_ge(tr_done, b + (BLOCKS + 1))
                nc.scalar.activation(hid_t[:, n, :], ps_h[:, bank, 0:P], ACT.Copy)
                nc.scalar.activation(hid_z[0:MUL1, n, :], ps_h[0:MUL1, bank, P:2 * P], ACT.Copy).then_inc(hidt_done, 1)

            def copy_block(b):
                nc.scalar.activation(fin_in[:, :, :], acc[:, :, bass.ds(b * P, P)], ACT.Copy).then_inc(fin_copied, 1)

            def windowed():
                def pair(k, first, finish):
                    for j in range(2 * G):
                        relu(k * (2 * G) + j, j % 2, first and j < 2)
                        if finish and j == 1:
                            normalize(k - LAG, 0)
                        if finish and j == 2:
                            move_block(k - LAG, 0, 1)
                        if finish and j == 3:
                            act.wait_ge(acc_done, k * (8 * G))
                            copy_block(k - LAG)

                pair(0, True, False)
                with act.Fori(1, LAG) as k:
                    pair(k, False, False)
                with act.Fori(LAG, PAIRS) as k:
                    pair(k, False, True)
                for j in range(LEFT):
                    relu((TURNS - 1) * G + j, j % 2, False)
                for n, b in enumerate(range(IN_LOOP, BLOCKS)):
                    normalize(b, n)
                    move_block(b, n, n)
                act.wait_ge(acc_done, 4 * (TURNS - 1) * G)
                act.wait_ge(fin_mm, IN_LOOP)
                copy_block(IN_LOOP)
                act.wait_ge(acc_done, 4 * EDGE_GROUPS)
                act.wait_ge(fin_mm, IN_LOOP + 1)
                copy_block(IN_LOOP + 1)

            def general():
                with act.Fori(0, GROUPS) as g:
                    act.wait_ge(g_fc1, g + 1)
                    nc.scalar.activation(hr[:, 0, :], ps_h[0:N_RADIAL, 0, 0:GE], ACT.Relu, scale=K_RADIAL).then_inc(g_relu, 1)

                act.wait_ge(g_block_free, BLOCKS + 1)
                normalize(0, 0)
                move_block(0, 0, 0)
                copy_block(0)
                with act.Fori(1, BLOCKS) as b:
                    act.wait_ge(fin_mm, b)
                    normalize(b, 0)
                    move_block(b, 0, 0)
                    copy_block(b)

            by_path(act, windowed, general)

        @block.vector
        def _(dve):
            def statistics(c, some):
                for b in some:
                    nc.vector.bn_stats(stats[:, b, :], xres[:, bass.ds(c * CHUNK + b, 1), :].rearrange("p b c -> p (b c)")).then_inc(bn_done, 1)

            def aggregate(c):
                dve.wait_ge(bn_done, c * CHUNK + CHUNK)
                dve.sem_inc(dve_passed, 1)
                for b in range(CHUNK):
                    ins = nc.vector.bn_aggr(mean_var[:, b, :], stats[:, b, :])
                ins.then_inc(aggr_done, 1)

            def normalizers(c):
                dve.wait_ge(std_done, c + 1)
                at = bass.ds(c * CHUNK, CHUNK)
                nc.vector.reciprocal(rstd[:, at], std[:, :]).then_inc(rstd_done, 1)
                dve.wait_ge(rstd_done, c + 1)
                nc.vector.scalar_tensor_tensor(shift[:, at], mean_var[:, :, 0], -1.0, rstd[:, at], ALU.mult, ALU.mult).then_inc(norm_done, 1)

            def take(c, parity, b, first):
                if not first and b == 0:
                    dve.wait_ge(table_out, c * 16 - 16)
                dve.wait_ge(node_mm, c * CHUNK + b + 1)
                nc.vector.tensor_scalar(l_st[:, parity, b, 0:Z], ps_w[:, b % 2, 0, 0:Z],
                                        a_sb[:, bass.ds(c * CHUNK + b, 1)], None, ALU.mult).then_inc(l_done, 1)

            def take_z(c, parity, q):
                dve.wait_ge(node_mm_z, c * 2 + q + 1)
                lo, hi = Z_BLOCKS[q]
                n = hi - lo
                nc.vector.tensor_tensor(l_st[:, parity, lo:hi, Z:C], ps_w[:, q, 2, 0:n * MUL1].rearrange("p (b u) -> p b u", u=MUL1),
                                        a_sb[:, bass.ds(c * CHUNK + lo, n)].unsqueeze(2).to_broadcast([P, n, MUL1]),
                                        ALU.mult).then_inc(lz_done, 1)

            dve.wait_ge(ld_x, 16)
            statistics(0, range(CHUNK))
            aggregate(0)
            dve.wait_ge(ld_wnode, 32)
            for part, scale in ((wl[:, 0:MUL0], MUL0 ** -0.5), (wl[:, MUL0:P], MUL1 ** -0.5), (wlz[:, :], MUL1 ** -0.5)):
                nc.vector.tensor_scalar(part, part, float(scale), None, ALU.mult).then_inc(w_scaled, 1)
            normalizers(0)

            dve.wait_ge(ld_a, 16)
            dve.wait_ge(ld_dst, 16)
            nc.vector.tensor_copy(base_i[:, :], dst_i[0:1, 0:TILES:T])
            nc.vector.tensor_copy(base_f[:, :], dst_i[0:1, 0:TILES:T]).then_inc(dst_step, 1)

            def scale_more():
                dve.wait_ge(ld_w, 80)
                for part, scale in ((wself[:, 0:MUL0], MUL0 ** -0.5), (wself[:, MUL0:P], MUL1 ** -0.5),
                                    (wselfz[:, :], MUL1 ** -0.5), (w_out[0:3 * MUL1, 3, :], K_SUM),
                                    (w_out[:, 0:3, :], K_SUM), (w_out[3 * MUL1:P, 3, :], K_SUM * K_DOT)):
                    nc.vector.tensor_scalar(part, part, float(scale), None, ALU.mult).then_inc(w_scaled, 1)

            def distances():
                dve.wait_ge(base_bc, 1)
                dve.wait_ge(dst_step, 2)
                by_group = dst_rel[:, :].rearrange("p (g t) -> p g t", t=T)
                nc.vector.tensor_tensor(by_group, by_group, base_ps[:, 0:GROUPS].unsqueeze(2).to_broadcast([P, GROUPS, T]),
                                        ALU.subtract).then_inc(dst_step, 1)

            def farthest():
                dve.wait_ge(dst_step, 3)
                nc.vector.tensor_reduce(span[:, 0:1], dst_rel[:, :], AX.X, ALU.max).then_inc(dst_step, 1)

            def nearest():
                nc.vector.tensor_reduce(span[:, 1:2], dst_rel[:, :], AX.X, ALU.min).then_inc(dst_step, 1)

            def lowest():
                dve.wait_ge(order_step, 3)
                nc.vector.tensor_reduce(span[:, 2:3], above, AX.X, ALU.min).then_inc(dst_step, 1)

            def outside():
                dve.wait_ge(dst_step, 6)
                nc.vector.tensor_scalar(span[:, 3:4], span[:, 0:1], float(W) - 0.5, None, ALU.is_gt).then_inc(dst_step, 1)
                nc.vector.tensor_scalar(span[:, 4:6], span[:, 1:3], -0.5, None, ALU.is_lt).then_inc(dst_step, 1)

            def chunk(c, parity, first, last, between={}):
                if not last:
                    dve.wait_ge(ld_x, c * 16 + 32)
                for b in range(CHUNK):
                    if not last:
                        if b == 0:
                            statistics(c + 1, range(0, 4))
                        if b == 1:
                            statistics(c + 1, range(4, CHUNK))
                        if b == 2:
                            aggregate(c + 1)
                        if b == 4:
                            normalizers(c + 1)
                    take(c, parity, b, first)
                    if b == 4:
                        take_z(c, parity, 0)
                    if b in between:
                        between[b]()
                take_z(c, parity, 1)

            def to_float():
                nc.vector.tensor_copy(dst_rel[:, :], dst_i[:, :]).then_inc(dst_step, 1)

            chunk(0, 0, True, False, {0: to_float, 2: distances, 5: scale_more})
            chunk(1, 1, True, False, {0: farthest, 2: nearest, 3: lowest, 5: outside})
            with dve.Fori(1, CHUNKS // 2) as t:
                for parity in range(2):
                    chunk(t * 2 + parity, parity, False, False)
            chunk(CHUNKS - 1, (CHUNKS - 1) % 2, False, True)
            dve.wait_ge(flag_sum, 1)
            nc.vector.tensor_copy(flag_i[:, :], flag_ps).then_inc(flag_set, 1)
            dve.wait_ge(consts, 9)
            dve.wait_ge(zeroed, 1)

            def attr_of(j, a, b):
                return attr_sb[:, j // HALF, (j % HALF) * T:(j % HALF) * T + T, a:b]

            def edge_dots(j):
                nc.vector.tensor_tensor(dots[:, :, :, :], vectors(j), attr_of(j, 1, 4).unsqueeze(3).to_broadcast([P, T, 3, MUL1]),
                                        ALU.mult).then_inc(dots_done, 1)

            def sum_dots():
                nc.vector.tensor_reduce(dot[:, :, :], dots[:, :, :, :].rearrange("p t d u -> p t u d"), AX.X, ALU.add).then_inc(dot_done, 1)

            def vectors(j):
                return y[:, j, :, MUL0:C].rearrange("p t (d u) -> p t d u", d=3)

            def scalar_products(j, s):
                nc.vector.tensor_tensor(msg[:, s, :, 0:2 * MUL0].rearrange("p t (k u) -> p t k u", k=2),
                                        ps_w[:, s, :, 0:2 * MUL0].rearrange("p t (k u) -> p t k u", k=2),
                                        y[:, j, :, 0:MUL0].unsqueeze(2).to_broadcast([P, T, 2, MUL0]), ALU.mult).then_inc(msg_done, 1)

            def vector_products(j, s):
                nc.vector.tensor_tensor(msg[:, s, :, 2 * MUL0:M - MUL1].rearrange("p t (d u) -> p t d u", d=3),
                                        ps_w[:, s, :, 2 * MUL0:NW - MUL1].unsqueeze(2).to_broadcast([P, T, 3, MUL1]),
                                        vectors(j), ALU.mult).then_inc(msg_done, 1)

            def dot_products(s):
                nc.vector.tensor_tensor(msg[:, s, :, M - MUL1:M], ps_w[:, s, :, NW - MUL1:NW], dot[:, :, :], ALU.mult).then_inc(msg_done, 1)

            def messages(i, j):
                g, s = i * G + j, j % 2
                if j % HALF == 0:
                    dve.wait_ge(ld_attr[j // HALF], i * 16 + 16)
                nc.vector.tensor_tensor(hot[:, s, :, 0, :], iota_w[:, :].unsqueeze(1).to_broadcast([P, T, W]),
                                        dst_rel[:, bass.ds(g * T, T)].unsqueeze(2).to_broadcast([P, T, W]),
                                        ALU.is_equal).then_inc(hot_done, 1)
                dve.wait_ge(gathered[j], i * (16 * T) + 16 * T)
                edge_dots(j)
                dve.wait_ge(hot_done, g + 1)
                nc.vector.tensor_tensor(hot[:, s, :, 1:V, :], hot[:, s, :, 0:1, :].to_broadcast([P, T, 4, W]),
                                        attr_of(j, 0, 4).unsqueeze(3).to_broadcast([P, T, 4, W]), ALU.mult).then_inc(msg_done, 1)
                dve.wait_ge(dots_done, g + 1)
                sum_dots()
                dve.wait_ge(fc2_done, g + 1)
                scalar_products(j, s)
                vector_products(j, s)
                dve.wait_ge(dot_done, g + 1)
                dot_products(s)

            def finish(b, frm):
                xr = xres[:, bass.ds(b, 1), :].rearrange("p b c -> p (b c)")
                nc.vector.scalar_tensor_tensor(xr, frm, a_sb[:, bass.ds(b, 1)], xr, ALU.mult, ALU.add).then_inc(fin_done, 1)

            def accumulate(g, s, base, first, block=None):
                dve.wait_ge(win_done, g + 1)
                if block is not None:
                    finish(block, ps_s[:, s, FIN:FIN + C])
                if not first:
                    dve.wait_ge(acc_done, g * 4)
                p = ps_s[:, s, :]
                for rows, slots, cols in ((slice(0, MUL0), slice(0, 1), slice(0, W)),
                                          (slice(MUL0, P), slice(0, 3), slice(W, 4 * W)),
                                          (slice(0, 3 * MUL1), slice(3, 4), slice(5 * W, 6 * W)),
                                          (slice(3 * MUL1, P), slice(3, 4), slice(4 * W, 5 * W))):
                    to = acc[rows, slots, bass.ds(base, W)]
                    nc.vector.tensor_tensor(to, to, p[rows, cols].rearrange("p (v n) -> p v n", n=W), ALU.add).then_inc(acc_done, 1)

            def base_of(g):
                return dve.value_load(base_i[0:1, bass.ds(g, 1)], min_val=0, max_val=N - 1)

            def windowed():
                def pair(k, first, last_of_block):
                    for j in range(2 * G):
                        g = k * (2 * G) + j
                        messages(k * 2 + j // G, j % G)
                        if j >= 1 or not first:
                            accumulate(g - 1, (j - 1) % 2, base_of(g - 1), first and j == 1,
                                       k - LAG if last_of_block and j == 6 else None)

                pair(0, True, False)
                with dve.Fori(1, LAG) as k:
                    pair(k, False, False)
                with dve.Fori(LAG, PAIRS) as k:
                    pair(k, False, True)
                for j in range(LEFT):
                    g = (TURNS - 1) * G + j
                    messages(TURNS - 1, j)
                    accumulate(g - 1, (g - 1) % 2, base_of(g - 1), False)
                dve.wait_ge(fin_mm, IN_LOOP + 1)
                finish(IN_LOOP, last_products(IN_LOOP))
                accumulate(EDGE_GROUPS - 1, (EDGE_GROUPS - 1) % 2, base_of(EDGE_GROUPS - 1), False)
                dve.wait_ge(fin_mm, BLOCKS)
                finish(IN_LOOP + 1, last_products(IN_LOOP + 1))

            def general():
                nc.vector.memset(full, 0.0)
                dve.sem_inc(g_free, 1)
                with dve.Fori(0, GROUPS) as g:
                    dve.wait_ge(g_loaded, g * 48 + 48)
                    dve.wait_ge(g_rows, g * (16 * T) + 16 * T)
                    edge_dots(0)
                    dve.drain()
                    sum_dots()
                    dve.wait_ge(g_fc2, g + 1)
                    scalar_products(0, 0)
                    vector_products(0, 0)
                    dve.drain()
                    dot_products(0)
                    for t in range(T):
                        n = g * T + t
                        nc.vector.tensor_copy(dst_col[:, :], dst_i[:, bass.ds(n, 1)])
                        dve.drain()
                        nc.vector.tensor_copy(dst_bc, dst_col[:, :].to_broadcast([P, P])).then_inc(g_col, 1)
                        dve.drain()
                        part = msg[:, 0, t, :]
                        for at, frm, k in ((0, slice(0, MUL0), 0), (MUL0, slice(MUL0, 2 * MUL0), 1),
                                           (P + MUL0, slice(MUL0, 2 * MUL0), 2), (2 * P + MUL0, slice(MUL0, 2 * MUL0), 3),
                                           (3 * P, slice(2 * MUL0, M - MUL1), 0)):
                            nc.vector.tensor_scalar(full[:, at:at + frm.stop - frm.start], part[:, frm],
                                                    attr_sb[:, 0, t, k:k + 1], None, ALU.mult)
                        nc.vector.tensor_copy(full[:, 4 * P - MUL1:4 * P], part[:, M - MUL1:M])
                        dve.wait_ge(g_turned, n + 1)
                        nc.vector.tensor_tensor(same, ps_s[:, 0, 0:P], dst_col[:, :].to_broadcast([P, P]), ALU.is_equal)
                        dve.drain()
                        dve.sem_inc(g_full, 1)
                        nc.vector.tensor_tensor(same_before, same, lower[:, :], ALU.mult)
                        nc.vector.tensor_tensor(away[:, :], trash[:, :], dst_col[:, :], ALU.subtract)
                        dve.drain()
                        nc.vector.tensor_reduce(repeats[:, :], same_before, AX.X, ALU.max)
                        dve.drain()
                        nc.vector.tensor_tensor(away[:, :], away[:, :], repeats[:, :], ALU.mult)
                        dve.drain()
                        dve.wait_ge(g_turn, n + 1)
                        nc.vector.tensor_tensor(idx_sum[:, :], away[:, :], dst_col[:, :], ALU.add)
                        dve.wait_ge(g_summed, n + 1)
                        nc.vector.tensor_copy(sums, ps_s[:, 1, :])
                        dve.drain()
                        dve.sem_inc(g_taken, 1)
                    dve.sem_inc(g_free, 1)
                dve.sem_inc(g_block_free, 1)
                with dve.Fori(0, BLOCKS) as b:
                    dve.wait_ge(g_block_turned, b + 1)
                    nc.vector.tensor_copy(acc[:, :, bass.ds(b * P, P)], ps_w[:, 0, :, 0:P]).then_inc(g_block_free, 1)
                with dve.Fori(0, BLOCKS) as b:
                    dve.wait_ge(fin_mm, b + 1)
                    finish(b, ps_w[:, 0, 0, 0:C])

            by_path(dve, windowed, general)

        @block.tensor
        def _(pe):
            pe.wait_ge(consts, 9)

            def had_bank(b):
                return b - 2 if b >= 2 else -1 - b

            def turn(c, b, first=False):
                pe.wait_ge(hid_done, c * CHUNK + b + 1)
                if not first:
                    pe.wait_ge(hidt_done, c * CHUNK + had_bank(b) + 1)
                nc.tensor.transpose(ps_h[:, b % 2, 0:P], hid[:, b, 0:P], ident[:, :]).then_inc(tr_done, 1)

            def chunk(c, first, last):
                def turn_z(q):
                    if not first:
                        pe.wait_ge(hidz_done, c * 2 + q - 1)
                    lo, hi = Z_BLOCKS[q]
                    nc.tensor.transpose(ps_s[0:(hi - lo) * MUL1, q, 0:P], hid_zs[:, lo * MUL1:hi * MUL1], ident[:, :]).then_inc(trz_done, 1)

                def linear(b):
                    pe.wait_ge(hidt_done, c * CHUNK + b + 1)
                    if b >= 2 or not first:
                        pe.wait_ge(l_done, c * CHUNK + had_bank(b) + 1)
                    nc.tensor.matmul(ps_w[:, b % 2, 0, 0:P], hid_t[:, b, :], wl[:, :], start=True, stop=True).then_inc(node_mm, 1)

                def linear_z(q):
                    pe.wait_ge(hidz_done, c * 2 + q + 1)
                    if first and q == 0:
                        pe.wait_ge(dst_step, 3)
                    if not first:
                        pe.wait_ge(lz_done, c * 2 + q - 1)
                    rows = MUL1 * (Z_BLOCKS[q][1] - Z_BLOCKS[q][0])
                    nc.tensor.matmul(ps_w[:, q, 2, 0:rows], hid_z[0:rows, q, :], wlz[0:rows, 0:rows],
                                     start=True, stop=True).then_inc(node_mm_z, 1)

                for b in range(CHUNK):
                    if b < CHUNK - 1:
                        turn(c, b + 1, first and b == 0)
                    elif not last:
                        turn(c + 1, 0)
                    if b in (2, CHUNK - 2):
                        turn_z(0 if b == 2 else 1)
                    if first and b == 0:
                        pe.wait_ge(dst_step, 1)
                        nc.tensor.matmul(base_ps[:, 0:GROUPS], ones[0:1, :], base_f[:, :], start=True, stop=True).then_inc(base_bc, 1)
                        pe.wait_ge(w_scaled, 3)
                    linear(b)
                    if b == 4:
                        linear_z(0)
                linear_z(1)

            turn(0, 0, True)
            chunk(0, True, False)
            with pe.Fori(1, CHUNKS - 1) as c:
                chunk(c, False, False)
            chunk(CHUNKS - 1, False, True)
            pe.wait_ge(dst_step, 8)
            pe.wait_ge(lz_done, 2 * CHUNKS)
            for n in range(3):
                ins = nc.tensor.matmul(flag_ps, ones[:, 0:1], span[:, 3 + n:4 + n], start=(n == 0), stop=(n == 2))
            ins.then_inc(flag_sum, 1)
            pe.wait_ge(w_scaled, 9)

            def fc1(i, j):
                if j % HALF == 0:
                    pe.wait_ge(ld_rad[j // HALF], i * 16 + 16)
                nc.tensor.matmul(ps_h[0:N_RADIAL, j % 2, 0:GE], w_fc1[:, :], rad[:, j // HALF, (j % HALF) * GE:(j % HALF + 1) * GE],
                                 start=True, stop=True).then_inc(fc1_done, 1)

            def fc2(g, s):
                pe.wait_ge(relu_done, g + 1)
                for t in range(T):
                    ins = nc.tensor.matmul(ps_w[:, s, t, 0:NW], hr[:, s, t * P:(t + 1) * P], w_fc2[:, :], start=True, stop=True)
                ins.then_inc(fc2_done, 1)

            def turn_block(b, n, bank):
                pe.wait_ge(hid_done, b + (BLOCKS + 1))
                nc.tensor.transpose(ps_h[:, bank, 0:P], hid[:, n, 0:P], ident[:, :])
                nc.tensor.transpose(ps_h[0:MUL1, bank, P:2 * P], hid_zs[:, n * MUL1:(n + 1) * MUL1], ident[:, :]).then_inc(tr_done, 1)

            def last_linear(b, n, o):
                pe.wait_ge(fin_copied, b + 1)
                nc.tensor.matmul(o[:, 0:C], fin_in[:, 3, :], w_out[:, 3, :], start=True, stop=False)
                nc.tensor.matmul(o[:, 0:MUL0 + MUL1], fin_in[:, 0, :], w_out[:, 0, 0:MUL0 + MUL1], start=False, stop=False)
                for d in (1, 2):
                    at = slice(MUL0 + MUL1 * d, MUL0 + MUL1 * (d + 1))
                    nc.tensor.matmul(o[:, at], fin_in[:, d, :], w_out[:, d, at], start=False, stop=False)
                nc.tensor.matmul(o[:, 0:Z], hid_t[:, n, :], wself[:, :], start=False, stop=False)
                nc.tensor.matmul(o[:, Z:C], hid_z[0:MUL1, n, :], wselfz[:, :], start=False, stop=True).then_inc(fin_mm, 1)

            def windows(g, s, first, block=None):
                pe.wait_ge(msg_done, g * 4 + 4)
                if not first:
                    pe.wait_ge(acc_done, (g - 1) * 4)
                if block is not None:
                    last_linear(block, 0, ps_s[:, s, FIN:FIN + C])
                for t in range(T):
                    nc.tensor.matmul(ps_s[:, s, 0:4 * W], msg[:, s, t, 0:P], hot[:, s, t, 1:V, :], start=(t == 0), stop=(t == T - 1))
                for t in range(T):
                    ins = nc.tensor.matmul(ps_s[:, s, 4 * W:6 * W], msg[:, s, t, P:M], hot[:, s, t, 0:2, :], start=(t == 0), stop=(t == T - 1))
                ins.then_inc(win_done, 1)

            def node_stage_left():
                pe.wait_ge(l_done, BLOCKS)
                pe.wait_ge(lz_done, 2 * CHUNKS)

            def windowed():
                def pair(k, first, finish):
                    for j in range(2 * G):
                        g = k * (2 * G) + j
                        if finish and j == 3:
                            pe.wait_ge(hidt_done, k - LAG + (BLOCKS + 1))
                        fc1(k * 2 + j // G, j % G)
                        if first and j == 1:
                            node_stage_left()
                        if j >= 1 or not first:
                            fc2(g - 1, (j - 1) % 2)
                        if finish and j == 2:
                            turn_block(k - LAG, 0, 1)
                        if j >= 2 or not first:
                            windows(g - 2, j % 2, first and j < 4, k - LAG if finish and j == 7 else None)

                pair(0, True, False)
                with pe.Fori(1, LAG) as k:
                    pair(k, False, False)
                with pe.Fori(LAG, PAIRS) as k:
                    pair(k, False, True)
                for j in range(LEFT):
                    g = (TURNS - 1) * G + j
                    fc1(TURNS - 1, j)
                    fc2(g - 1, (g - 1) % 2)
                    windows(g - 2, g % 2, False)
                last = EDGE_GROUPS - 1
                fc2(last, last % 2)
                for n, b in enumerate(range(IN_LOOP, BLOCKS)):
                    turn_block(b, n, n)
                windows(last - 1, (last - 1) % 2, False)
                last_linear(IN_LOOP, 0, last_products(IN_LOOP))
                windows(last, last % 2, False)
                last_linear(IN_LOOP + 1, 1, last_products(IN_LOOP + 1))

            def general():
                node_stage_left()
                with pe.Fori(0, GROUPS) as g:
                    pe.wait_ge(g_loaded, g * 48 + 48)
                    nc.tensor.matmul(ps_h[0:N_RADIAL, 0, 0:GE], w_fc1[:, :], rad[:, 0, 0:GE], start=True, stop=True).then_inc(g_fc1, 1)
                    pe.wait_ge(g_relu, g + 1)
                    for t in range(T):
                        ins = nc.tensor.matmul(ps_w[:, 0, t, 0:NW], hr[:, 0, t * P:(t + 1) * P], w_fc2[:, :], start=True, stop=True)
                    ins.then_inc(g_fc2, 1)
                    for t in range(T):
                        n = g * T + t
                        pe.wait_ge(g_col, n + 1)
                        nc.tensor.transpose(ps_s[:, 0, 0:P], dst_bc, ident[:, :]).then_inc(g_turned, 1)
                        pe.wait_ge(g_full, n + 1)
                        nc.tensor.matmul(ps_s[:, 1, :], same, full, start=True, stop=True).then_inc(g_summed, 1)
                with pe.Fori(0, BLOCKS) as b:
                    pe.wait_ge(g_block_in, b * 16 + 16)
                    for v in range(4):
                        ins = nc.tensor.transpose(ps_w[:, 0, v, 0:P], rows_in[:, v * P:(v + 1) * P], ident[:, :])
                    ins.then_inc(g_block_turned, 1)

                turn_block(0, 0, 0)
                last_linear(0, 0, ps_w[:, 0, 0, :])
                with pe.Fori(1, BLOCKS) as b:
                    turn_block(b, 0, 0)
                    pe.wait_ge(fin_done, b)
                    last_linear(b, 0, ps_w[:, 0, 0, :])

            by_path(pe, windowed, general)


ORDER = np.concatenate([np.arange(MUL0)] + [MUL0 + 3 * np.arange(MUL1) + d for d in range(3)])


def kernel(**inputs):
    import concourse.bacc as bacc
    from concourse.bass_utils import run_bass_kernel_spmd

    get = {k: np.asarray(v) for k, v in inputs.items()}

    def by_tile(v, fill):
        padded = np.concatenate([v, np.broadcast_to(fill, (EP - E, *v.shape[1:])).astype(v.dtype)])
        return np.ascontiguousarray(np.moveaxis(padded.reshape(TILES, P, *v.shape[1:]), 0, 1))

    def padded_rows(v):
        return np.concatenate([v, np.zeros((NP - N, v.shape[1]), v.dtype)])

    radial = np.zeros((N_BASIS, EP), np.float32)
    radial[:, :E] = get["edge_attr_10"].T
    arrays = {
        "x": np.ascontiguousarray(padded_rows(get["x"])[:, ORDER]),
        "src": by_tile(get["src"], 0),
        "dst": by_tile(get["dst"], get["dst"][-1]),
        "radial": radial,
        "attr": by_tile(get["edge_attr_4"], 0),
        "avec": np.ascontiguousarray(padded_rows(get["node_vec1"]).reshape(BLOCKS, P).T),
    }
    w = {k[7:]: v for k, v in get.items() if k.startswith("L0_gnn_")}
    w_lin, w_self, w_lin_z = (np.zeros((P, P), np.float32) for _ in range(3))
    w_last = np.zeros((P, 4, C), np.float32)
    w_last[:MUL0, 0, :MUL0] = w["W_l2_00"]
    w_last[3 * MUL1:, 3, :MUL0] = w["W_l2_10"]
    for whole, w0, w1 in ((w_lin, "W_l1_0", "W_l1_1"), (w_self, "W_si0", "W_si1")):
        whole[:MUL0, :MUL0] = w[w0]
        for d in range(2):
            at = slice(MUL0 + MUL1 * d, MUL0 + MUL1 * (d + 1))
            whole[at, at] = w[w1]
    for b in range(P // MUL1):
        at = slice(MUL1 * b, MUL1 * (b + 1))
        w_lin_z[at, at] = w["W_l1_1"]
    for d in range(3):
        at = slice(MUL0 + MUL1 * d, MUL0 + MUL1 * (d + 1))
        w_last[MUL0:, d, at] = w["W_l2_01"]
        w_last[MUL1 * d:MUL1 * (d + 1), 3, at] = w["W_l2_11"]
    arrays["w_lin"], arrays["w_lin_z"], arrays["w_self"] = w_lin, w_lin_z, w_self
    arrays["w_self_z"] = np.ascontiguousarray(w["W_si1"])
    arrays["w_last"] = w_last
    arrays["w_fc1"] = np.ascontiguousarray(w["W_fc1"])
    arrays["w_fc2"] = np.ascontiguousarray(w["W_fc2"])
    nc = bacc.Bacc("TRN2", target_bir_lowering=False, num_devices=1)
    args = [nc.dram_tensor(f"in_{k}", a.shape, mybir.dt.from_np(a.dtype), kind="ExternalInput").ap() for k, a in arrays.items()]
    args.append(nc.dram_tensor("out", (NP, C), F32, kind="ExternalOutput").ap())
    gnn_layer(nc, *args)
    r = run_bass_kernel_spmd(nc, [{f"in_{k}": a for k, a in arrays.items()}], core_ids=[0])
    rows = np.asarray(r.results[0]["out"])[:N]
    result = np.empty_like(rows)
    result[:, ORDER] = rows
    return result
```
